# Optimizing a Trainium2 kernel written in Bass

```python
import numpy as np
import jax
import jax.numpy as jnp

def _softmax(x, axis=-1):
    return jax.nn.softmax(x, axis=axis)

def _gelu(x):
    return jax.nn.gelu(x, approximate=True)

def _silu(x):
    return jax.nn.silu(x)

def _sigmoid(x):
    return jax.nn.sigmoid(x)

def _layernorm(x, axis=-1, eps=1e-05):
    m = jnp.mean(x, axis=axis, keepdims=True)
    v = jnp.var(x, axis=axis, keepdims=True)
    return (x - m) / jnp.sqrt(v + eps)

def _scatter_add(tgt, idx, src, axis=0):
    return tgt.at[idx].add(src)

def _segment_sum(src, seg, n):
    return jax.ops.segment_sum(src, seg, n)
kernel_name = 'mk_adaln_ffn_d1_seqx_r4_f331c0'

def setup_inputs(seed: int=0):
    np.random.seed(seed)
    _w = jnp.asarray

    def _rec_inputs():
        import jax
        import jax.numpy as jnp
        _rk = jax.random.key(seed)
        x = -7.109e-05 + 0.9999 * jax.random.normal(jax.random.fold_in(_rk, 1), (16, 256, 256), jnp.float32)
        _lenS = 256 - jax.random.randint(jax.random.fold_in(_rk, 7), (16,), 0, max(1, 256 // 4) + 1, jnp.int32)
        _lenS2 = 256 - jax.random.randint(jax.random.fold_in(_rk, 8), (16,), 0, max(1, 256 // 4) + 1, jnp.int32)
        cond_1024 = 0.00386106 + 1.00199 * jax.random.normal(jax.random.fold_in(_rk, 11), (16, 256), jnp.float32)
        return (x, cond_1024)
    x, cond_1024 = _rec_inputs()

    def _L0_cond_setup():
        import jax, jax.numpy as jnp
        import numpy as np
        import math
        IN_F = 256
        OUT_F = 256
        B = 16
        L = 1024
        key = jax.random.key(seed)
        k1, k2, k3 = jax.random.split(key, 3)
        Efou = jax.random.normal(k1, (B, L, IN_F), dtype=jnp.float32)
        y = jax.random.normal(k2, (B, IN_F), dtype=jnp.float32)
        weight = jax.random.normal(k3, (1, OUT_F, IN_F, 1), dtype=jnp.float32)
        return {'Efou': Efou, 'y': y, 'weight': weight}
    _L0_cond_all = _L0_cond_setup()
    _L0_cond_in = {k: v for k, v in _L0_cond_all.items() if k in ('weight',)}
    del _L0_cond_all

    def _L0_ffn_setup():
        import jax, jax.numpy as jnp
        import numpy as np
        NUM_EXPERTS = 8
        TOP_K = 2
        key = jax.random.key(seed)
        ks = jax.random.split(key, 6)
        B, S, D, F = (2, 512, 256, 1024)
        E = NUM_EXPERTS
        sd = 1.0 / np.sqrt(D)
        sf = 1.0 / np.sqrt(F)
        return {'x': jax.random.normal(ks[0], (B, S, D), dtype=jnp.float32), 'gate_w': jax.random.normal(ks[1], (E, D), dtype=jnp.float32) * sd, 'w1': jax.random.uniform(ks[2], (F, E, D), dtype=jnp.float32, minval=-sd, maxval=sd), 'b1': jax.random.uniform(ks[3], (E, F), dtype=jnp.float32, minval=-sd, maxval=sd), 'w2': jax.random.uniform(ks[4], (D, E, F), dtype=jnp.float32, minval=-sf, maxval=sf), 'b2': jax.random.uniform(ks[5], (E, D), dtype=jnp.float32, minval=-sf, maxval=sf)}
    _L0_ffn_all = _L0_ffn_setup()
    _L0_ffn_in = {k: v for k, v in _L0_ffn_all.items() if k in ('gate_w', 'w1', 'b1', 'w2', 'b2')}
    del _L0_ffn_all
    return {'x': x, 'cond_1024': cond_1024, 'L0_cond_weight': _L0_cond_in['weight'], 'L0_ffn_gate_w': _L0_ffn_in['gate_w'], 'L0_ffn_w1': _L0_ffn_in['w1'], 'L0_ffn_b1': _L0_ffn_in['b1'], 'L0_ffn_w2': _L0_ffn_in['w2'], 'L0_ffn_b2': _L0_ffn_in['b2']}

def reference(x, cond_1024, L0_cond_weight, L0_ffn_gate_w, L0_ffn_w1, L0_ffn_b1, L0_ffn_w2, L0_ffn_b2):
    import jax
    import jax.numpy as jnp

    def _L0_cond_ref(Efou, y, weight):
        import jax, jax.numpy as jnp
        import numpy as np
        import math
        IN_F = 256
        OUT_F = 256
        B = 16
        L = 1024
        b, img_size, in_f = Efou.shape
        out_f = weight.shape[1]
        scale = 1.0 / math.sqrt(in_f)
        w = scale * weight[:, :, :, 0] * y[:, None, :]
        dnorm = jax.lax.rsqrt(jnp.sum(w * w, axis=2, keepdims=True) + 1e-08)
        w = w * dnorm
        E = Efou.reshape(b, in_f, img_size)
        x = jnp.einsum('boi,bil->bol', w, E)
        return x.reshape(b, img_size, out_f)

    def _L0_ffn_ref(x, gate_w, w1, b1, w2, b2):
        import jax, jax.numpy as jnp
        import numpy as np
        NUM_EXPERTS = 8
        TOP_K = 2
        logits = jnp.einsum('bsd,ed->bse', x, gate_w)
        probs = jax.nn.softmax(logits, axis=-1)
        topk_probs, topk_idx = jax.lax.top_k(probs, TOP_K)
        oh = jax.nn.one_hot(topk_idx, NUM_EXPERTS, dtype=x.dtype)
        h = jnp.einsum('bsd,fed,bske->bskf', x, w1, oh)
        h = h + jnp.take(b1, topk_idx, axis=0)
        h = jax.nn.gelu(h)
        y = jnp.einsum('bskf,def,bske->bskd', h, w2, oh)
        y = y + jnp.take(b2, topk_idx, axis=0)
        out = jnp.sum(y * topk_probs[..., None], axis=-2)
        return out
    x = x + _L0_ffn_ref(_L0_cond_ref(x, cond_1024, L0_cond_weight), L0_ffn_gate_w, L0_ffn_w1, L0_ffn_b1, L0_ffn_w2, L0_ffn_b2)
    return x

_drawn_inputs = setup_inputs


def setup_inputs(seed=0):
    import zlib

    import numpy as np

    out = dict(_drawn_inputs(seed))
    spreads = {}
    factors = {'L0_ffn_b1': 8.0, 'L0_ffn_b2': 6.725}
    for name, (base, spread) in spreads.items():
        noise = np.random.default_rng([zlib.crc32(name.encode()), seed]).standard_normal(out[name].shape)
        drawn = base * np.exp(spread * noise) if base else spread * noise
        out[name] = jnp.asarray(drawn.astype(out[name].dtype))
    for name, factor in factors.items():
        out[name] = (out[name] * factor).astype(out[name].dtype)
    return out
```

```python
from contextlib import ExitStack

import concourse.bass as bass
from concourse import mybir

P = 128
ALU = mybir.AluOpType
ACT = mybir.ActivationFunctionType
AX = mybir.AxisListType
F32 = mybir.dt.float32
F16 = mybir.dt.float16
BF16 = mybir.dt.bfloat16
I32 = mybir.dt.int32
F16_MAX = 65504.0
VERY_LOW = -3.0e38


def moe_kernel(nc, x, x_t, y_t, cond_w_t, gate_w_t, w1, b1, w2, b2, out):
    B, S, D = x.shape
    E = gate_w_t.shape[2]
    F = w1.shape[3]
    IC = S // P
    DC = D // P
    FC = F // P
    T = B * S
    Q = T // P
    HALF = FC // 2
    TOP = 2
    MOST = (TOP * T + E * (P - 1)) // P
    TILES = -(-MOST // 4) * 4
    ROW = D + E
    W1C = DC * F
    WC = W1C + FC * D
    GROUP = 4
    NG = B // GROUP
    PAIRS = B // 2
    RING = 4
    COND_SCALE = 1.0 / float(S) ** 0.5

    with ExitStack() as ctx:

        def sb(name, shape, dt):
            return ctx.enter_context(nc.sbuf_tensor(name, shape, dt))

        def sem(name):
            return ctx.enter_context(nc.semaphore(name))

        w_hi = sb("w_hi", [P, E * WC], F16)
        w_lo = sb("w_lo", [P, E * WC], BF16)
        xt_sb = w_hi[:, E // 2 * WC:].bitcast(F32).rearrange("p (c b i) -> p c b i", c=DC, b=B)
        x_sb = w_lo[:, E // 2 * WC:].bitcast(F32).rearrange("p (c b l) -> p c b l", c=IC, b=B)
        HOTS = (E // 2 - 1) * WC
        J = TOP * Q

        def hots(start, n):
            return w_hi[:, HOTS + J * start:HOTS + J * (start + n)].bitcast(BF16).rearrange(
                "p (j n) -> p j n", n=n)

        hi_tile, lo_hot, hi_hot = hots(0, TILES), hots(TILES, P), hots(TILES + P, TILES)
        STAGES = 3
        stage = sb("stage", [P, STAGES, W1C], F32)

        x_rows = sb("x_rows", [P, RING, ROW], F32)
        x_hi = sb("x_hi", [P, 2, DC * P], F16)
        x_lo = sb("x_lo", [P, 2, DC * P], BF16)
        gates = sb("gates", [P, RING, 1], F32)
        act_h = sb("act_h", [P, 2, F], F32)
        h_area = sb("h_area", [P, 2 * IC * 2 * ROW], F32)
        h_parts = h_area[:, 0:2 * F].bitcast(F16).rearrange("p (k a n) -> p k a n", k=2, a=2)
        y_sum = sb("y_sum", [P, 2, D], F32)
        y_out = sb("y_out", [P, RING, D], F32)
        gather_at = sb("gather_at", [P, RING], I32)
        scatter_at = sb("scatter_at", [P, RING], I32)
        b1_sb = sb("b1_sb", [P, E * FC], F32)
        b2_sb = sb("b2_sb", [P, E * D], F32)
        xs = act_h[:, :, :].rearrange("p k (c n) -> p k c n", c=IC)
        rows_out = h_area[:, :].rearrange("p (k c j n) -> p k c j n", k=2, c=IC, j=2)

        cw = sb("cw", [P, IC, S], F32)
        cw_sq = y_out[:, 0:IC, :]
        gw = sb("gw", [P, DC, E], F32)
        y_sb = sb("y_sb", [P, IC, B], F32)
        y_sq = sb("y_sq", [P, IC, B], F32)
        yg = sb("yg", [P, IC, B, E], F32)
        norm = sb("norm", [P, IC, B], F32)
        root = sb("root", [P, IC, B], F32)
        newton = sb("newton", [P, IC, B], F32)
        dn = sb("dn", [P, IC, B], F32)

        logits = sb("logits", [P, Q, E], F32)
        probs = sb("probs", [P, Q, E], F32)
        tmp = sb("tmp", [P, Q, E], F32)
        first = sb("first", [P, Q, E], F32)
        second = sb("second", [P, Q, E], F32)
        both = sb("both", [P, E, Q], BF16)
        top = sb("top", [P, Q], F32)
        pick = sb("pick", [P, Q], F32)
        total = sb("total", [P, Q], F32)
        g_all = sb("g_all", [P, Q, E], F32)
        upto = sb("upto", [P, E, Q], F32)
        slot_e = sb("slot_e", [P, E, Q], F32)
        count_i = sb("count_i", [P, E], I32)
        n_tiles = sb("n_tiles", [P, E], F32)
        end_tile = sb("end_tile", [P, E], F32)
        base = sb("base", [P, E], F32)
        slots = sb("slots", [P, TOP, Q], F32)
        slots_i = sb("slots_i", [P, TOP * Q], I32)
        part_i = sb("part_i", [P, 2, TOP * Q], I32)
        part_f = sb("part_f", [P, 2, TOP * Q], F32)
        empty = sb("empty", [P, TILES], F32)
        rows_of = sb("rows_of", [P, TILES], I32)
        ended = x_rows[0:1, 0:2, :].rearrange("p s n -> p (s n)")[:, 0:TILES * (E - 1)].rearrange(
            "p (t e) -> p t e", e=E - 1)
        expert_of_f = sb("expert_of_f", [1, TILES], F32)
        expert_of = sb("expert_of", [1, TILES], I32)

        ident = sb("ident", [P, P], F32)
        before = sb("before", [P, P], BF16)
        ones_bf = sb("ones_bf", [P, P], BF16)
        ones = sb("ones", [P, E], F32)
        zero_row = y_sum[:, :, :].rearrange("p k n -> p (k n)")[:, 0:ROW]
        rev = sb("rev", [P, E], F32)
        col = sb("col", [P, P], F32)
        row = sb("row", [P, 1], F32)
        tile_at = sb("tile_at", [P, Q], F32)
        not_first = sb("not_first", [P, E, Q], F32)

        rows_dram = nc.dram_tensor("rows_dram", [T + P, ROW], F32, kind="Internal").ap()

        bank = [ctx.enter_context(nc.psum_tensor(f"bank{i}", [P, 512], F32)) for i in range(8)]
        ps_g = bank[0][:, 0:IC * B * E].rearrange("p (c b e) -> p c b e", c=IC, b=B)
        ps_norm = bank[1][:, 0:IC * B].rearrange("p (c b) -> p c b", c=IC)
        ps_log = bank[2][:, 0:IC * B * E].rearrange("p (c n) -> p c n", c=IC)
        ps_before = bank[3][:, 0:E * Q]
        ps_count = bank[3][:, E * Q:2 * E * Q]
        ps_rows = bank[1][:, 128:128 + TILES]
        ps_cond = [[bank[4 + 2 * k + c] for c in range(IC)] for k in range(2)]
        ps_h = [[bank[2 * k][:, :], bank[2 * k + 1][:, :]] for k in range(2)]
        ps_xt = [bank[4 + k][:, 0:DC * P] for k in range(2)]
        ps_y = [bank[6 + k][:, 0:D] for k in range(2)]

        small_in = sem("small_in")
        xt_in = [sem(f"xt_in{i}") for i in range(NG)]
        x_in = [sem(f"x_in{i}") for i in range(NG)]
        bias_in = sem("bias_in")
        w_in = [sem(f"w_in{i}") for i in range(STAGES)]
        stage_free = sem("stage_free")
        head_done = sem("head_done")
        consts_ready = sem("consts_ready")
        pool_step = sem("pool_step")
        dve_step = sem("dve_step")
        sq_ready = sem("sq_ready")
        norm_done = sem("norm_done")
        norm_ready = sem("norm_ready")
        root_ready = sem("root_ready")
        g_done = sem("g_done")
        yg_ready = sem("yg_ready")
        logits_done = sem("logits_done")
        dn_ready = sem("dn_ready")
        shifted_ready = sem("shifted_ready")
        exp_ready = sem("exp_ready")
        gates_ready = sem("gates_ready")
        xs_ready = sem("xs_ready")
        cond_done = sem("cond_done")
        cond_out = sem("cond_out")
        gates_put = sem("gates_put")
        rows_stored = [sem(f"rows_stored{k}") for k in range(2)]
        pad_stored = sem("pad_stored")
        out_set = sem("out_set")
        both_ready = sem("both_ready")
        prefix_done = sem("prefix_done")
        hots_ready = sem("hots_ready")
        slots_done = sem("slots_done")
        tables_ready = sem("tables_ready")

        pool_passed = sem("pool_passed")
        picked = sem("picked")
        gathered = [sem(f"gathered{s}") for s in range(RING)]
        turned = sem("turned")
        x_head = sem("x_head")
        x_ready = sem("x_ready")
        hidden = sem("hidden")
        gelu_done = sem("gelu_done")
        h_head = sem("h_head")
        h_ready = sem("h_ready")
        down_done = sem("down_done")
        y_taken = sem("y_taken")
        y_ready = sem("y_ready")
        added = sem("added")

        block = ctx.enter_context(nc.Block())

        def half(t, e, k, n=None):
            return t[:, e * WC + k * W1C:e * WC + (k + 1) * W1C]

        @block.sync
        def _(sp):
            sp.dma_start(cw[:, :, :], cond_w_t.rearrange("c p o -> p c o")).then_inc(small_in, 16)
            sp.dma_start(gw[:, :, :], gate_w_t.rearrange("c p e -> p c e")).then_inc(small_in, 16)
            sp.dma_start(y_sb[:, :, :], y_t.rearrange("c p b -> p c b")).then_inc(small_in, 16)
            for g in range(NG):
                b = slice(g * GROUP, (g + 1) * GROUP)
                for c in range(DC):
                    sp.dma_start(xt_sb[:, c, b, :], x_t[b, c * P:(c + 1) * P, :].rearrange(
                        "b p i -> p b i")).then_inc(xt_in[g], 16)
            for g in range(NG):
                b = slice(g * GROUP, (g + 1) * GROUP)
                for c in range(IC):
                    sp.dma_start(x_sb[:, c, b, :], x[b, c * P:(c + 1) * P, :].rearrange(
                        "b p l -> p b l")).then_inc(x_in[g], 16)
            sp.dma_start(b1_sb[:, :], b1).then_inc(bias_in, 16)
            sp.dma_start(b2_sb[:, :], b2.partition_broadcast(P)).then_inc(bias_in, 16)
            for n in range(2 * E):
                if n >= STAGES:
                    sp.wait_ge(stage_free, n - STAGES + 1)
                src = (w1, w2)[n % 2][n // 2].rearrange("p a b -> p (a b)")
                sp.dma_start(stage[:, n % STAGES, :], src).then_inc(w_in[n % STAGES], 16)

        @block.gpsimd
        def _(pool):
            steps = [0]

            def step(ins):
                steps[0] += 1
                ins.then_inc(pool_step, 1)
                pool.wait_ge(pool_step, steps[0])

            pool.memset(ident[:, :], 0.0)
            pool.memset(ones_bf[:, :], 1.0)
            pool.memset(ones[:, :], 1.0)
            pool.memset(not_first[:, :, :], 1.0)
            step(pool.memset(zero_row, 0.0))
            pool.iota(col[:, :], [[1, P]], base=0, channel_multiplier=0,
                      allow_small_or_imprecise_dtypes=True)
            pool.iota(row[:, :], [[0, 1]], base=0, channel_multiplier=1,
                      allow_small_or_imprecise_dtypes=True)
            pool.iota(tile_at[:, :], [[P, IC], [S, B]], base=-T, channel_multiplier=0,
                      allow_small_or_imprecise_dtypes=True)
            pool.iota(rev[:, :], [[-1, E]], base=E, channel_multiplier=0,
                      allow_small_or_imprecise_dtypes=True)
            pool.memset(not_first[:, :, 0:1], 0.0)
            pool.affine_select(out=ident[:, :], in_=ident[:, :], compare_op=ALU.not_equal, fill=1.0,
                               base=0, pattern=[[-1, P]], channel_multiplier=1)
            step(pool.affine_select(out=before[:, :], in_=ones_bf[:, :], compare_op=ALU.is_gt,
                                    fill=0.0, base=0, pattern=[[1, P]], channel_multiplier=-1))
            pool.memset(gates[:, :, :], 0.0).then_inc(consts_ready, 1)
            pool.wait_ge(small_in, 48)
            for n in range(PAIRS):
                if n % 2 == 0:
                    pool.wait_ge(x_in[n // 2], 16 * IC)
                if n >= 2:
                    pool.wait_ge(cond_done, n - 1)
                for c in range(IC):
                    for k in range(2):
                        b = 2 * n + k
                        last = pool.tensor_scalar(xs[:, n % 2, c, k * D:(k + 1) * D],
                                                  x_sb[:, c, b, :], y_sb[:, c, b:b + 1], 1.0,
                                                  ALU.mult, ALU.mult)
                last.then_inc(xs_ready, 1)

            def pick_rows(to, table_col, s):
                return pool.tensor_copy(to[:, s:s + 1], rows_of[:, table_col])

            def carry_wait():
                pool.sem_inc(pool_passed, 1)

            def gather(s):
                pool.indirect_dma_start(
                    out=x_rows[:, s, :], out_offset=None, in_=rows_dram,
                    in_offset=bass.IndirectOffsetOnAxis(ap=gather_at[:, s:s + 1].bitcast(mybir.dt.uint32), axis=0),
                ).then_inc(gathered[s], 16)

            pool.wait_ge(tables_ready, 1)
            pool.wait_ge(rows_stored[0], 16 * IC * (PAIRS // 2))
            pool.wait_ge(rows_stored[1], 16 * IC * (PAIRS // 2))
            pool.wait_ge(pad_stored, 32)
            for s in range(RING):
                pick_rows(gather_at, slice(s, s + 1), s).then_inc(picked, 1)
            pool.wait_ge(picked, RING)
            for s in range(RING):
                gather(s)
            pool.wait_ge(out_set, 16 * IC * NG)

            def round_of(r, more):
                for s in range(RING):
                    t = r * RING + s
                    at = bass.ds(t, 1)
                    pick_rows(scatter_at, at, s).then_inc(picked, 1)
                    if more:
                        pool.wait_ge(gathered[s], 16 * (r + 1))
                        pool.wait_ge(x_ready, t + 1)
                        pick_rows(gather_at, bass.ds(t + RING, 1), s).then_inc(picked, 1)
                        pool.wait_ge(picked, RING + 2 * t + 2)
                        carry_wait()
                        gather(s)
                    else:
                        pool.wait_ge(picked, RING + 2 * (TILES - RING) + s + 1)
                    pool.wait_ge(y_ready, t + 1)
                    if not isinstance(t, int) or t > 0:
                        pool.wait_ge(added, 16 * t)
                        carry_wait()
                    pool.indirect_dma_start(
                        out=out, out_offset=bass.IndirectOffsetOnAxis(ap=scatter_at[:, s:s + 1].bitcast(mybir.dt.uint32), axis=0),
                        in_=y_out[:, s, :], in_offset=None, compute_op=ALU.add,
                    ).then_inc(added, 16)

            round_of(0, True)
            with pool.Fori(1, TILES // RING - 1) as r:
                round_of(r, True)
            round_of(TILES // RING - 1, False)
            pool.wait_ge(added, 16 * TILES)

        @block.scalar
        def _(act):
            act.wait_ge(consts_ready, 1)
            act.dma_start(rows_dram[T:T + P, :], zero_row).then_inc(pad_stored, 16)
            act.dma_start(out[T:T + P, :], zero_row[:, 0:D]).then_inc(pad_stored, 16)
            act.wait_ge(norm_ready, 1)
            nc.scalar.activation(root[:, :, :], norm[:, :, :], ACT.Sqrt).then_inc(root_ready, 1)
            act.wait_ge(shifted_ready, 1)
            nc.scalar.activation(probs[:, :, :], tmp[:, :, :], ACT.Exp).then_inc(exp_ready, 1)
            act.wait_ge(dn_ready, 1)
            for n in range(PAIRS):
                k = n % 2
                act.wait_ge(cond_done, n + 1)
                if n >= 2:
                    act.wait_ge(rows_stored[k], 16 * IC * (n // 2))
                for c in range(IC):
                    for j in range(2):
                        b = 2 * n + j
                        last = nc.scalar.activation(rows_out[:, k, c, j, 0:D],
                                                    ps_cond[k][c][:, j * D:(j + 1) * D],
                                                    ACT.Copy, scale=dn[:, c, b:b + 1])
                last.then_inc(cond_out, 1)
                if n == 0:
                    for g in range(NG):
                        act.wait_ge(x_in[g], 16 * IC)
                        for c in range(IC):
                            b = slice(g * GROUP, (g + 1) * GROUP)
                            act.dma_start(
                                out[0:T, :].rearrange("(b c p) l -> c p b l", b=B, c=IC)[c][:, b, :],
                                x_sb[:, c, b, :]).then_inc(out_set, 16)
                act.wait_ge(cond_out, n + 1)
                act.wait_ge(gates_put, n + 1)
                for c in range(IC):
                    dst = rows_dram[0:T, :].rearrange("(b c p) l -> c p b l", b=B, c=IC)
                    ins = act.dma_start(dst[c][:, 2 * n:2 * n + 2, :], rows_out[:, k, c, :, :])
                    ins.then_inc(rows_stored[k], 16)
            act.wait_ge(bias_in, 32)
            act.wait_ge(tables_ready, 1)

            def gelu_tile(t, k):
                e = act.value_load(expert_of[0:1, bass.ds(t, 1)], min_val=0, max_val=E - 1)
                for f in range(FC):
                    if f % HALF == 0:
                        act.wait_ge(hidden, 2 * t + f // HALF + 1)
                    if f == 0 and not (isinstance(t, int) and t < 2):
                        act.wait_ge(h_ready, 2 * t - 2)
                    nc.scalar.activation(
                        act_h[:, k, f * P:(f + 1) * P],
                        ps_h[k][f // 4][:, f % 4 * P:(f % 4 + 1) * P], ACT.Gelu_apprx_tanh,
                        bias=b1_sb[:, bass.ds(e * FC + f, 1)]).then_inc(gelu_done, 1)

            for t in range(2):
                gelu_tile(t, t)
            with act.Fori(1, TILES // 2) as r:
                for k in range(2):
                    gelu_tile(r * 2 + k, k)

        @block.vector
        def _(dve):
            steps = [0]

            def step(ins):
                steps[0] += 1
                ins.then_inc(dve_step, 1)
                dve.wait_ge(dve_step, steps[0])

            v = nc.vector

            def over_e(ap):
                return ap.unsqueeze(2).to_broadcast([P, Q, E])

            dve.wait_ge(small_in, 48)
            v.tensor_tensor(cw_sq[:, :, :], cw[:, :, :], cw[:, :, :], ALU.mult)
            v.tensor_tensor(y_sq[:, :, :], y_sb[:, :, :], y_sb[:, :, :], ALU.mult).then_inc(sq_ready, 1)
            dve.wait_ge(norm_done, 1)
            v.tensor_scalar(norm[:, :, :], ps_norm, COND_SCALE * COND_SCALE, 1e-8,
                            ALU.mult, ALU.add).then_inc(norm_ready, 1)
            dve.wait_ge(root_ready, 1)
            step(v.reciprocal(dn[:, :, :], root[:, :, :]))
            step(v.tensor_tensor(newton[:, :, :], dn[:, :, :], dn[:, :, :], ALU.mult))
            step(v.tensor_tensor(newton[:, :, :], newton[:, :, :], norm[:, :, :], ALU.mult))
            step(v.tensor_scalar(newton[:, :, :], newton[:, :, :], -0.5 * COND_SCALE,
                                 1.5 * COND_SCALE, ALU.mult, ALU.add))
            steps[0] += 1
            v.tensor_tensor(dn[:, :, :], dn[:, :, :], newton[:, :, :], ALU.mult).then_inc(dve_step, 1)
            dve.wait_ge(dve_step, steps[0])
            dve.wait_ge(g_done, 1)
            v.tensor_tensor(yg[:, :, :, :], ps_g,
                            y_sb[:, :, :].unsqueeze(3).to_broadcast([P, IC, B, E]),
                            ALU.mult).then_inc(yg_ready, 1)
            dve.wait_ge(logits_done, 1)
            dn_q = dn[:, :, :].rearrange("p c b -> p (c b)")
            dve.wait_ge(consts_ready, 1)
            step(v.tensor_tensor(logits[:, :, :], ps_log.rearrange("p c (b e) -> p (c b) e", e=E),
                                 over_e(dn_q), ALU.mult))
            rev_q = rev[:, :].unsqueeze(1).to_broadcast([P, Q, E])
            step(v.tensor_reduce(top[:, :], logits[:, :, :], AX.X, ALU.max))
            v.tensor_tensor(tmp[:, :, :], logits[:, :, :], over_e(top[:, :]),
                            ALU.subtract).then_inc(shifted_ready, 1)
            step(v.tensor_tensor(first[:, :, :], logits[:, :, :], over_e(top[:, :]), ALU.is_equal))
            step(v.tensor_tensor(first[:, :, :], first[:, :, :], rev_q, ALU.mult))
            step(v.tensor_reduce(pick[:, :], first[:, :, :], AX.X, ALU.max))
            step(v.tensor_tensor(first[:, :, :], over_e(pick[:, :]), rev_q, ALU.is_equal))
            step(v.scalar_tensor_tensor(logits[:, :, :], first[:, :, :], VERY_LOW, logits[:, :, :],
                                        ALU.mult, ALU.add))
            step(v.tensor_reduce(top[:, :], logits[:, :, :], AX.X, ALU.max))
            step(v.tensor_tensor(second[:, :, :], logits[:, :, :], over_e(top[:, :]), ALU.is_equal))
            step(v.tensor_tensor(second[:, :, :], second[:, :, :], rev_q, ALU.mult))
            step(v.tensor_reduce(pick[:, :], second[:, :, :], AX.X, ALU.max))
            step(v.tensor_tensor(second[:, :, :], over_e(pick[:, :]), rev_q, ALU.is_equal))
            v.tensor_tensor(both[:, :, :].rearrange("p e q -> p q e"), first[:, :, :],
                            second[:, :, :], ALU.add).then_inc(both_ready, 1)
            dve.wait_ge(exp_ready, 1)
            step(v.tensor_reduce(total[:, :], probs[:, :, :], AX.X, ALU.add))
            step(v.reciprocal(total[:, :], total[:, :]))
            step(v.tensor_tensor(tmp[:, :, :], first[:, :, :], second[:, :, :], ALU.add))
            step(v.tensor_tensor(tmp[:, :, :], tmp[:, :, :], probs[:, :, :], ALU.mult))
            step(v.tensor_tensor(g_all[:, :, :], tmp[:, :, :], over_e(total[:, :]), ALU.mult))
            v.tensor_copy(empty[:, 0:1], ones[:, 0:1]).then_inc(dn_ready, 1)
            g_v = g_all[:, :, :].rearrange("p (c b) e -> p c b e", c=IC)

            def put_gates(n):
                if n >= 2:
                    dve.wait_ge(rows_stored[n % 2], 32 * (n // 2))
                v.tensor_copy(rows_out[:, n % 2, :, :, D:ROW],
                              g_v[:, :, 2 * n:2 * n + 2, :]).then_inc(gates_put, 1)

            put_gates(0)
            put_gates(1)
            dve.wait_ge(prefix_done, 1)
            count = ps_count.rearrange("p (e q) -> p e q", e=E)
            step(v.tensor_tensor_scan(upto[:, :, :].rearrange("p e q -> p (e q)"),
                                      not_first[:, :, :].rearrange("p e q -> p (e q)"),
                                      ps_count, 0.0, ALU.mult, ALU.add))
            step(v.tensor_scalar(count_i[:, :], upto[:, :, Q - 1], float(P - 1), None, ALU.add))
            step(v.tensor_scalar(count_i[:, :], count_i[:, :], 7, None, ALU.logical_shift_right))
            step(v.tensor_copy(n_tiles[:, :], count_i[:, :]))
            step(v.tensor_tensor_scan(end_tile[:, :], ones[:, :], n_tiles[:, :], 0.0,
                                      ALU.mult, ALU.add))
            step(v.tensor_tensor(base[:, :], end_tile[:, :], n_tiles[:, :], ALU.subtract))
            step(v.tensor_tensor(slot_e[:, :, :], upto[:, :, :], count, ALU.subtract))
            step(v.tensor_tensor(slot_e[:, :, :], slot_e[:, :, :],
                                 ps_before.rearrange("p (e q) -> p e q", e=E), ALU.add))
            step(v.scalar_tensor_tensor(slot_e[:, :, :],
                                        base[:, :].unsqueeze(2).to_broadcast([P, E, Q]), float(P),
                                        slot_e[:, :, :], ALU.mult, ALU.add))
            slot_q = slot_e[:, :, :].rearrange("p e q -> p q e")
            for k, chosen in enumerate((first, second)):
                step(v.tensor_tensor(tmp[:, :, :], slot_q, chosen[:, :, :], ALU.mult))
                step(v.tensor_reduce(slots[:, k, :], tmp[:, :, :], AX.X, ALU.add))
            step(v.tensor_copy(slots_i[:, :], slots[:, :, :].rearrange("p k q -> p (k q)")))
            v.tensor_scalar(part_i[:, 0, :], slots_i[:, :], 7, None, ALU.logical_shift_right)
            step(v.tensor_scalar(part_i[:, 1, :], slots_i[:, :], P - 1, None, ALU.bitwise_and))
            step(v.tensor_copy(part_f[:, :, :], part_i[:, :, :]))
            put_gates(2)
            dve.wait_ge(g_done, 1)
            v.tensor_tensor(lo_hot, col[:, :].unsqueeze(1).to_broadcast([P, J, P]),
                            part_f[:, 1, :].unsqueeze(2).to_broadcast([P, J, P]), ALU.is_equal)
            put_gates(3)
            step(v.tensor_tensor(hi_hot, col[:, 0:TILES].unsqueeze(1).to_broadcast([P, J, TILES]),
                                 part_f[:, 0, :].unsqueeze(2).to_broadcast([P, J, TILES]),
                                 ALU.is_equal))
            for k in range(TOP):
                q = slice(k * Q, (k + 1) * Q)
                last = v.tensor_tensor(hi_tile[:, q, :], hi_hot[:, q, :],
                                       tile_at[:, :].unsqueeze(2).to_broadcast([P, Q, TILES]), ALU.mult)
            step(last)
            v.tensor_scalar(hi_hot, hi_hot, row[:, 0:1], None, ALU.mult).then_inc(hots_ready, 1)
            for n in range(4, PAIRS):
                put_gates(n)
            dve.wait_ge(slots_done, 1)
            step(v.tensor_scalar(empty[:, :], ps_rows, 0.0, row[:, 0:1], ALU.is_equal, ALU.mult))
            v.scalar_tensor_tensor(rows_of[:, :], ps_rows, float(T), empty[:, :], ALU.add, ALU.add)
            step(v.tensor_tensor(ended[:, :, :],
                                 end_tile[0:1, 0:E - 1].unsqueeze(1).to_broadcast([1, TILES, E - 1]),
                                 col[0:1, 0:TILES].unsqueeze(2).to_broadcast([1, TILES, E - 1]),
                                 ALU.is_le))
            step(v.tensor_reduce(expert_of_f[:, :], ended[:, :, :], AX.X, ALU.add))
            v.tensor_copy(expert_of[:, :], expert_of_f[:, :]).then_inc(tables_ready, 1)

            for n in range(2 * E):
                e, k, s = n // 2, n % 2, n % STAGES
                dve.wait_ge(w_in[s], 16 * (n // STAGES + 1))
                if n == E:
                    dve.wait_ge(xs_ready, PAIRS)
                    dve.wait_ge(out_set, 16 * IC * NG)
                v.tensor_scalar(half(w_hi, e, k), stage[:, s, :], F16_MAX, -F16_MAX,
                                ALU.min, ALU.max).then_inc(head_done, 1)
                dve.wait_ge(head_done, n + 1)
                v.tensor_tensor(half(w_lo, e, k), stage[:, s, :], half(w_hi, e, k),
                                ALU.subtract).then_inc(stage_free, 1)

            def split_x(t, s, k):
                e = dve.value_load(expert_of[0:1, bass.ds(t, 1)], min_val=0, max_val=E - 1)
                dve.wait_ge(turned, t + 1)
                if not (isinstance(t, int) and t < 2):
                    dve.wait_ge(hidden, 2 * (t - 1))
                v.tensor_scalar(x_hi[:, k, :], ps_xt[k], F16_MAX, -F16_MAX,
                                ALU.min, ALU.max).then_inc(x_head, 1)
                v.tensor_copy(gates[:, s, :], x_rows[:, s, bass.ds(D + e, 1)])
                dve.wait_ge(x_head, t + 1)
                v.tensor_tensor(x_lo[:, k, :], ps_xt[k], x_hi[:, k, :],
                                ALU.subtract).then_inc(x_ready, 1)

            def split_h(t, k):
                hf = F // 2
                h_lo = h_parts[:, k, 1, :].bitcast(BF16)
                for c in range(2):
                    dve.wait_ge(gelu_done, t * FC + FC // 2 * (c + 1))
                    if c == 0 and not (isinstance(t, int) and t < 2):
                        dve.wait_ge(down_done, t - 1)
                    f = slice(c * hf, (c + 1) * hf)
                    v.tensor_scalar(h_parts[:, k, 0, f], act_h[:, k, f], F16_MAX, -F16_MAX,
                                    ALU.min, ALU.max).then_inc(h_head, 1)
                for c in range(2):
                    f = slice(c * hf, (c + 1) * hf)
                    dve.wait_ge(h_head, 2 * t + c + 1)
                    v.tensor_tensor(h_lo[:, f], act_h[:, k, f], h_parts[:, k, 0, f],
                                    ALU.subtract).then_inc(h_ready, 1)

            def finish_y(t, s, k):
                e = dve.value_load(expert_of[0:1, bass.ds(t, 1)], min_val=0, max_val=E - 1)
                dve.wait_ge(down_done, t + 1)
                v.tensor_tensor(y_sum[:, k, :], ps_y[k], b2_sb[:, bass.ds(e * D, D)],
                                ALU.add).then_inc(y_taken, 1)
                dve.wait_ge(y_taken, t + 1)
                if not (isinstance(t, int) and t < RING):
                    dve.wait_ge(added, 16 * (t - RING + 1))
                v.tensor_scalar(y_out[:, s, :], y_sum[:, k, :], gates[:, s, 0:1], None,
                                ALU.mult).then_inc(y_ready, 1)

            def tile_step(t, s):
                split_h(t, s % 2)
                if not (isinstance(t, int) and t == 0):
                    finish_y(t - 1, (s - 1) % RING, (s - 1) % 2)
                if not (isinstance(t, int) and t + 2 >= TILES):
                    split_x(t + 2, (s + 2) % RING, s % 2)

            dve.wait_ge(bias_in, 32)
            for t in range(2):
                split_x(t, t, t)
            for t in range(RING):
                tile_step(t, t)
            with dve.Fori(1, TILES // RING - 1) as r:
                for s in range(RING):
                    tile_step(r * RING + s, s)
            for t in range(TILES - RING, TILES):
                tile_step(t, t % RING)
            finish_y(TILES - 1, RING - 1, 1)

        @block.tensor
        def _(pe):
            mm = nc.tensor.matmul
            pe.wait_ge(sq_ready, 1)
            for o in range(IC):
                for c in range(IC):
                    last = mm(ps_norm[:, o, :], cw_sq[:, c, o * P:(o + 1) * P], y_sq[:, c, :],
                              start=(c == 0), stop=(c == IC - 1))
            last.then_inc(norm_done, 1)
            for g in range(NG):
                pe.wait_ge(xt_in[g], 16 * DC)
                for b in range(g * GROUP, (g + 1) * GROUP):
                    for i in range(IC):
                        for c in range(DC):
                            last = mm(ps_g[:, i, b, :], xt_sb[:, c, b, i * P:(i + 1) * P],
                                      gw[:, c, :], start=(c == 0), stop=(c == DC - 1))
            last.then_inc(g_done, 1)
            pe.wait_ge(yg_ready, 1)
            for o in range(IC):
                for c in range(IC):
                    last = mm(ps_log[:, o, :], cw[:, c, o * P:(o + 1) * P],
                              yg[:, c, :, :].rearrange("p b e -> p (b e)"),
                              start=(c == 0), stop=(c == IC - 1))
            last.then_inc(logits_done, 1)

            def cond_pair(n):
                pe.wait_ge(xs_ready, n + 1)
                if n >= 2:
                    pe.wait_ge(cond_out, n - 1)
                for o in range(IC):
                    for c in range(IC):
                        last = mm(ps_cond[n % 2][o][:, :], cw[:, c, o * P:(o + 1) * P],
                                  xs[:, n % 2, c, :], start=(c == 0), stop=(c == IC - 1))
                last.then_inc(cond_done, 1)

            cond_pair(0)
            cond_pair(1)
            pe.wait_ge(both_ready, 1)
            pe.wait_ge(consts_ready, 1)
            both_f = both[:, :, :].rearrange("p e q -> p (e q)")
            mm(ps_before, before[:, :], both_f, start=True, stop=True)
            mm(ps_count, ones_bf[:, :], both_f, start=True, stop=True).then_inc(prefix_done, 1)
            for n in range(2, PAIRS):
                cond_pair(n)
            pe.wait_ge(hots_ready, 1)
            for j in range(J):
                for part in (hi_tile, hi_hot):
                    last = mm(ps_rows, lo_hot[:, j, :], part[:, j, :],
                              start=(j == 0 and part is hi_tile), stop=(j == J - 1 and part is hi_hot))
            last.then_inc(slots_done, 1)
            pe.wait_ge(tables_ready, 1)

            def turn(t, s, k):
                pe.wait_ge(gathered[s], 16 * (t // RING + 1) if isinstance(t, int) else t[1])
                n = t if isinstance(t, int) else t[0]
                if not (isinstance(n, int) and n < 2):
                    pe.wait_ge(x_ready, n - 1)
                for c in range(DC):
                    last = nc.tensor.transpose(ps_xt[k][:, c * P:(c + 1) * P],
                                               x_rows[:, s, c * P:(c + 1) * P], ident[:, :])
                last.then_inc(turned, 1)

            def up(t, k):
                e = pe.value_load(expert_of[0:1, bass.ds(t, 1)], min_val=0, max_val=E - 1)
                pe.wait_ge(x_ready, t + 1)
                if not (isinstance(t, int) and t < 2):
                    pe.wait_ge(gelu_done, FC * (t - 1))
                for f in range(FC):
                    to = ps_h[k][f // 4][:, f % 4 * P:(f % 4 + 1) * P]
                    for c in range(DC):
                        at = bass.ds(e * WC + (c * F + f * P), P)
                        xc = slice(c * P, (c + 1) * P)
                        mm(to, w_hi[:, at], x_hi[:, k, xc], start=(c == 0), stop=False)
                        mm(to, w_hi[:, at], x_lo[:, k, xc], start=False, stop=False)
                        last = mm(to, w_lo[:, at], x_hi[:, k, xc], start=False, stop=(c == DC - 1))
                    if f % HALF == HALF - 1:
                        last.then_inc(hidden, 1)

            def down(t, k):
                e = pe.value_load(expert_of[0:1, bass.ds(t, 1)], min_val=0, max_val=E - 1)
                if not (isinstance(t, int) and t < 2):
                    pe.wait_ge(y_taken, t - 1)
                h_hi = h_parts[:, k, 0, :]
                h_lo = h_parts[:, k, 1, :].bitcast(BF16)
                for f in range(FC):
                    if f % (FC // 2) == 0:
                        pe.wait_ge(h_ready, 2 * t + f // (FC // 2) + 1)
                    at = bass.ds(e * WC + (W1C + f * D), D)
                    fs = slice(f * P, (f + 1) * P)
                    mm(ps_y[k], h_hi[:, fs], w_hi[:, at], start=(f == 0), stop=False)
                    mm(ps_y[k], h_hi[:, fs], w_lo[:, at], start=False, stop=False)
                    last = mm(ps_y[k], h_lo[:, fs], w_hi[:, at], start=False, stop=(f == FC - 1))
                last.then_inc(down_done, 1)

            for t in range(2):
                turn(t, t, t)
            pe.wait_ge(stage_free, 2 * E)
            up(0, 0)

            def tile_step(t, s, r):
                if not (isinstance(t, int) and t + 1 >= TILES):
                    up(t + 1, (s + 1) % 2)
                if not (isinstance(t, int) and t + 2 >= TILES):
                    rounds = r + 1 if s + 2 < RING else r + 2
                    turn(t + 2 if isinstance(t, int) else (t + 2, 16 * rounds), (s + 2) % RING, s % 2)
                down(t, s % 2)

            for t in range(RING):
                tile_step(t, t, 0)
            with pe.Fori(1, TILES // RING - 1) as r:
                for s in range(RING):
                    tile_step(r * RING + s, s, r)
            for t in range(TILES - RING, TILES):
                tile_step(t, t % RING, TILES // RING - 1)


def kernel(x, cond_1024, L0_cond_weight, L0_ffn_gate_w, L0_ffn_w1, L0_ffn_b1, L0_ffn_w2, L0_ffn_b2):
    import numpy as np
    import concourse.bacc as bacc
    from concourse.bass_utils import run_bass_kernel_spmd

    x = np.asarray(x)
    B, S, D = x.shape
    E, F = L0_ffn_b1.shape
    w1, w2 = np.asarray(L0_ffn_w1), np.asarray(L0_ffn_w2)
    arrays = {
        "x": x,
        "x_t": x.transpose(0, 2, 1),
        "y_t": np.asarray(cond_1024).T.reshape(S // P, P, B),
        "cond_w_t": np.asarray(L0_cond_weight)[0, :, :, 0].T.reshape(S // P, P, S),
        "gate_w_t": np.asarray(L0_ffn_gate_w).T.reshape(D // P, P, E),
        "w1": w1.transpose(1, 2, 0).reshape(E, D // P, P, F).transpose(0, 2, 1, 3),
        "b1": np.asarray(L0_ffn_b1).reshape(E, F // P, P).transpose(2, 0, 1).reshape(P, -1),
        "w2": w2.transpose(1, 2, 0).reshape(E, F // P, P, D).transpose(0, 2, 1, 3),
        "b2": np.asarray(L0_ffn_b2).reshape(-1),
    }
    nc = bacc.Bacc("TRN2", target_bir_lowering=False, num_devices=1)
    ins, aps = {}, []
    for name, a in arrays.items():
        a = np.ascontiguousarray(a)
        ins[f"in_{name}"] = a
        aps.append(nc.dram_tensor(f"in_{name}", a.shape, mybir.dt.from_np(a.dtype),
                                  kind="ExternalInput").ap())
    out = nc.dram_tensor("out", (B * S + P, D), F32, kind="ExternalOutput").ap()
    moe_kernel(nc, *aps, out)
    got = run_bass_kernel_spmd(nc, [ins], core_ids=[0]).results[0]["out"]
    return got[:B * S].reshape(B, S, D)
```

```python
from contextlib import ExitStack

import concourse.bass as bass
from concourse import mybir

P = 128
ALU = mybir.AluOpType
ACT = mybir.ActivationFunctionType
AX = mybir.AxisListType
F32 = mybir.dt.float32
F16 = mybir.dt.float16
BF16 = mybir.dt.bfloat16
I32 = mybir.dt.int32
F16_MAX = 65504.0
VERY_LOW = -3.0e38


def moe_kernel(nc, x, x_t, y_t, cond_w_t, gate_w_t, w1, b1, w2, b2, out):
    B, S, D = x.shape
    E = gate_w_t.shape[2]
    F = w1.shape[3]
    IC = S // P
    DC = D // P
    FC = F // P
    T = B * S
    Q = T // P
    TOP = 2
    SUB = 2
    N = SUB * P
    TILES = (TOP * T + E * (N - 1)) // N
    U = TILES * SUB
    ROW = D + E
    W1C = DC * F
    WC = W1C + FC * D
    GROUP = 4
    NG = B // GROUP
    PAIRS = B // 2
    BF = 512 // N
    BANKS = FC // BF
    GW = 32
    COND_SCALE = 1.0 / float(S) ** 0.5

    with ExitStack() as ctx:

        def sb(name, shape, dt):
            return ctx.enter_context(nc.sbuf_tensor(name, shape, dt))

        def sem(name):
            return ctx.enter_context(nc.semaphore(name))

        w_hi = sb("w_hi", [P, E * WC], F16)
        w_lo = sb("w_lo", [P, E * WC], BF16)
        xt_sb = w_hi[:, E // 2 * WC:].bitcast(F32).rearrange("p (c b i) -> p c b i", c=DC, b=B)
        x_sb = w_lo[:, E // 2 * WC:].bitcast(F32).rearrange("p (c b l) -> p c b l", c=IC, b=B)
        HOTS = (E // 2 - 1) * WC
        J = TOP * Q

        def hots(start, n):
            return w_hi[:, HOTS + J * start:HOTS + J * (start + n)].bitcast(BF16).rearrange(
                "p (j n) -> p j n", n=n)

        hi_tile, lo_hot, hi_hot = hots(0, U), hots(U, P), hots(U + P, U)
        stage = sb("stage", [P, 2, W1C], F32)

        x_rows = sb("x_rows", [P, 2, SUB, ROW], F32)
        x_hi = sb("x_hi", [P, DC, N], F16)
        x_lo = sb("x_lo", [P, DC, N], BF16)
        gates = sb("gates", [P, 2, SUB, 1], F32)
        act_h = sb("act_h", [P, BANKS, BF * N], F32)
        h_area = sb("h_area", [P, 2 * IC * 2 * ROW], F32)
        h_hi = h_area[:, 0:F * SUB // 2].bitcast(F16).rearrange("p (f n) -> p f n", n=N)
        h_lo = h_area[:, F * SUB // 2:F * SUB].bitcast(BF16).rearrange("p (f n) -> p f n", n=N)
        y_sum = sb("y_sum", [P, SUB, D], F32)
        y_out = sb("y_out", [P, 2, SUB, D], F32)
        gather_at = sb("gather_at", [P, 2, SUB], I32)
        scatter_at = sb("scatter_at", [P, 2, SUB], I32)
        b1_sb = sb("b1_sb", [P, E * FC], F32)
        b2_sb = sb("b2_sb", [P, E * D], F32)
        xs = act_h[:, :, :].rearrange("p (k c) n -> p k c n", k=2)
        rows_out = h_area[:, :].rearrange("p (k c j n) -> p k c j n", k=2, c=IC, j=2)

        cw = sb("cw", [P, IC, S], F32)
        cw_sq = y_out[:, 0, :, :]
        gw = sb("gw", [P, DC, GW], F32)
        gt_sb = sb("gt_sb", [P, 2, 512], F32)
        y_sb = sb("y_sb", [P, IC, B], F32)
        y_sq = sb("y_sq", [P, IC, B], F32)
        yg = sb("yg", [P, IC, B, E], F32)
        norm = sb("norm", [P, IC, B], F32)
        root = sb("root", [P, IC, B], F32)
        newton = sb("newton", [P, IC, B], F32)
        dn = sb("dn", [P, IC, B], F32)

        logits = sb("logits", [P, Q, E], F32)
        probs = sb("probs", [P, Q, E], F32)
        tmp = sb("tmp", [P, Q, E], F32)
        first = sb("first", [P, Q, E], F32)
        second = sb("second", [P, Q, E], F32)
        both = sb("both", [P, E, Q], BF16)
        top = sb("top", [P, Q], F32)
        pick = sb("pick", [P, Q], F32)
        total = sb("total", [P, Q], F32)
        g_all = sb("g_all", [P, Q, E], F32)
        upto = sb("upto", [P, E, Q], F32)
        slot_e = sb("slot_e", [P, E, Q], F32)
        count_i = sb("count_i", [P, E], I32)
        n_tiles = sb("n_tiles", [P, E], F32)
        end_tile = sb("end_tile", [P, E], F32)
        base = sb("base", [P, E], F32)
        slots = sb("slots", [P, TOP, Q], F32)
        slots_i = sb("slots_i", [P, TOP * Q], I32)
        part_i = sb("part_i", [P, 2, TOP * Q], I32)
        part_f = sb("part_f", [P, 2, TOP * Q], F32)
        empty = sb("empty", [P, U], F32)
        rows_of = sb("rows_of", [P, U], I32)
        pad_row = sb("pad_row", [P, U], F32)
        ended = x_rows[0:1, 0, :, :].rearrange("p s n -> p (s n)")[:, 0:TILES * (E - 1)].rearrange(
            "p (t e) -> p t e", e=E - 1)
        expert_of_f = sb("expert_of_f", [1, TILES], F32)
        expert_of = sb("expert_of", [1, TILES], I32)

        ident = sb("ident", [P, P], F32)
        before = sb("before", [P, P], BF16)
        ones_bf = sb("ones_bf", [P, P], BF16)
        ones = sb("ones", [P, E], F32)
        zero_row = y_sum[:, :, :].rearrange("p s n -> p (s n)")[:, 0:ROW]
        rev = sb("rev", [P, E], F32)
        col = sb("col", [P, P], F32)
        row = sb("row", [P, 1], F32)
        tile_at = sb("tile_at", [P, Q], F32)
        not_first = sb("not_first", [P, E, Q], F32)

        rows_dram = nc.dram_tensor("rows_dram", [T + N, ROW], F32, kind="Internal").ap()

        bank = [ctx.enter_context(nc.psum_tensor(f"bank{i}", [P, 512], F32)) for i in range(8)]
        ps_gt = [bank[h] for h in range(2)]
        ps_g = [bank[2 + h][:, :].rearrange("p (b c j e) -> p b c j e", b=2, c=IC, j=4) for h in range(2)]
        ps_norm = bank[3][:, 0:IC * B].rearrange("p (c b) -> p c b", c=IC)
        ps_log = bank[0][:, 0:IC * B * E].rearrange("p (c n) -> p c n", c=IC)
        ps_before = bank[1][:, 0:E * Q]
        ps_count = bank[1][:, E * Q:2 * E * Q]
        ps_rows = bank[2][:, 0:U]
        ps_cond = [[bank[4 + 2 * k + c] for c in range(IC)] for k in range(2)]
        ps_h = [bank[j] for j in range(BANKS)]
        ps_xt = bank[4][:, 0:DC * N]
        ps_y = [bank[6 + m][:, 0:D] for m in range(SUB)]

        small_in = sem("small_in")
        xt_in = [sem(f"xt_in{i}") for i in range(NG)]
        x_in = [sem(f"x_in{i}") for i in range(NG)]
        bias_in = sem("bias_in")
        w_in = [sem(f"w_in{i}") for i in range(2)]
        gw_set = sem("gw_set")
        head_done = sem("head_done")
        rest_done = sem("rest_done")
        consts_ready = sem("consts_ready")
        pool_step = sem("pool_step")
        dve_step = sem("dve_step")
        sq_ready = sem("sq_ready")
        norm_done = sem("norm_done")
        norm_ready = sem("norm_ready")
        root_ready = sem("root_ready")
        gt_done = sem("gt_done")
        gt_taken = sem("gt_taken")
        g_done = sem("g_done")
        yg_ready = sem("yg_ready")
        logits_done = sem("logits_done")
        dn_ready = sem("dn_ready")
        shifted_ready = sem("shifted_ready")
        exp_ready = sem("exp_ready")
        gates_ready = sem("gates_ready")
        xs_ready = sem("xs_ready")
        cond_done = sem("cond_done")
        cond_out = sem("cond_out")
        gates_put = sem("gates_put")
        rows_stored = [sem(f"rows_stored{k}") for k in range(2)]
        pad_stored = sem("pad_stored")
        out_set = sem("out_set")
        both_ready = sem("both_ready")
        prefix_done = sem("prefix_done")
        hots_ready = sem("hots_ready")
        slots_done = sem("slots_done")
        tables_ready = sem("tables_ready")

        pool_passed = sem("pool_passed")
        picked = sem("picked")
        gathered = [sem(f"gathered{s}") for s in range(2)]
        turned = sem("turned")
        x_head = sem("x_head")
        x_ready = sem("x_ready")
        hidden = sem("hidden")
        gelu_done = sem("gelu_done")
        h_head = sem("h_head")
        h_ready = sem("h_ready")
        down_done = sem("down_done")
        y_taken = sem("y_taken")
        y_ready = sem("y_ready")
        added = sem("added")

        FIRST = E - 1
        ROUNDS = (TILES - 2 - FIRST) // 2
        assert FIRST + 2 * ROUNDS + 2 == TILES

        block = ctx.enter_context(nc.Block())

        def half(t, e, k):
            return t[:, e * WC + k * W1C:e * WC + (k + 1) * W1C]

        @block.sync
        def _(sp):
            sp.wait_ge(gw_set, 1)
            sp.dma_start(gw[:, :, 0:E], gate_w_t.rearrange("c p e -> p c e")).then_inc(small_in, 16)
            sp.dma_start(y_sb[:, :, :], y_t.rearrange("c p b -> p c b")).then_inc(small_in, 16)
            sp.dma_start(cw[:, :, :], cond_w_t.rearrange("c p o -> p c o")).then_inc(small_in, 16)

            def samples(g):
                return slice(g * GROUP, (g + 1) * GROUP)

            def load_x(g):
                for c in range(IC):
                    sp.dma_start(x_sb[:, c, samples(g), :], x[samples(g), c * P:(c + 1) * P, :].rearrange(
                        "b p l -> p b l")).then_inc(x_in[g], 16)

            def load_w(e):
                for k in range(2):
                    if e > 0:
                        sp.wait_ge(rest_done, 2 * (e - 1) + k + 1)
                    src = (w1, w2)[k][e].rearrange("p a b -> p (a b)")
                    sp.dma_start(stage[:, k, :], src).then_inc(w_in[k], 16)

            for g in range(NG):
                for c in range(DC):
                    sp.dma_start(xt_sb[:, c, samples(g), :], x_t[samples(g), c * P:(c + 1) * P, :].rearrange(
                        "b p i -> p b i")).then_inc(xt_in[g], 16)
            load_x(0)
            load_w(0)
            for g in range(1, NG):
                load_x(g)
            sp.dma_start(b1_sb[:, :], b1).then_inc(bias_in, 16)
            sp.dma_start(b2_sb[:, :], b2.partition_broadcast(P)).then_inc(bias_in, 16)
            for g in range(NG):
                sp.wait_ge(x_in[g], 16 * IC)
                for c in range(IC):
                    sp.dma_start(
                        out[0:T, :].rearrange("(b c p) l -> c p b l", b=B, c=IC)[c][:, samples(g), :],
                        x_sb[:, c, samples(g), :]).then_inc(out_set, 16)
            for e in range(1, E):
                load_w(e)

        @block.gpsimd
        def _(pool):
            steps = [0]

            def step(ins):
                steps[0] += 1
                ins.then_inc(pool_step, 1)
                pool.wait_ge(pool_step, steps[0])

            pool.memset(gw[:, :, :], 0.0).then_inc(gw_set, 1)
            pool.memset(ident[:, :], 0.0)
            pool.memset(ones_bf[:, :], 1.0)
            pool.memset(ones[:, :], 1.0)
            pool.memset(not_first[:, :, :], 1.0)
            step(pool.memset(zero_row, 0.0))
            pool.iota(col[:, :], [[1, P]], base=0, channel_multiplier=0,
                      allow_small_or_imprecise_dtypes=True)
            pool.iota(row[:, :], [[0, 1]], base=0, channel_multiplier=1,
                      allow_small_or_imprecise_dtypes=True)
            pool.iota(tile_at[:, :], [[P, IC], [S, B]], base=-T, channel_multiplier=0,
                      allow_small_or_imprecise_dtypes=True)
            pool.iota(pad_row[:, :], [[0, TILES], [P, SUB]], base=0, channel_multiplier=1,
                      allow_small_or_imprecise_dtypes=True)
            pool.iota(rev[:, :], [[-1, E]], base=E, channel_multiplier=0,
                      allow_small_or_imprecise_dtypes=True)
            pool.memset(not_first[:, :, 0:1], 0.0)
            pool.affine_select(out=ident[:, :], in_=ident[:, :], compare_op=ALU.not_equal, fill=1.0,
                               base=0, pattern=[[-1, P]], channel_multiplier=1)
            step(pool.affine_select(out=before[:, :], in_=ones_bf[:, :], compare_op=ALU.is_gt,
                                    fill=0.0, base=0, pattern=[[1, P]], channel_multiplier=-1))
            pool.memset(gates[:, :, :, :], 0.0).then_inc(consts_ready, 1)
            pool.wait_ge(small_in, 48)
            def scale_pair(n):
                if n % 2 == 0:
                    pool.wait_ge(x_in[n // 2], 16 * IC)
                if n >= 2:
                    pool.wait_ge(cond_done, n - 1)
                for c in range(IC):
                    for k in range(2):
                        b = 2 * n + k
                        last = pool.tensor_scalar(xs[:, n % 2, c, k * D:(k + 1) * D],
                                                  x_sb[:, c, b, :], y_sb[:, c, b:b + 1], 1.0,
                                                  ALU.mult, ALU.mult)
                last.then_inc(xs_ready, 1)

            def rest_of(e, k):
                pool.wait_ge(head_done, 2 * e + k + 1)
                pool.tensor_tensor(half(w_lo, e, k), stage[:, k, :], half(w_hi, e, k),
                                   ALU.subtract).then_inc(rest_done, 1)

            for n in range(PAIRS):
                scale_pair(n)
                if n == 4:
                    rest_of(0, 0)
                if n == 6:
                    rest_of(0, 1)

            def pick_rows(to, t, s):
                pool.tensor_copy(to[:, s, :], rows_of[:, bass.ds(t * SUB, SUB)]).then_inc(picked, 1)

            def numbers(ap):
                return bass.IndirectOffsetOnAxis(ap=ap.bitcast(mybir.dt.uint32), axis=0)

            def gather(s):
                for m in range(SUB):
                    pool.indirect_dma_start(
                        out=x_rows[:, s, m, :], out_offset=None, in_=rows_dram,
                        in_offset=numbers(gather_at[:, s, m:m + 1])).then_inc(gathered[s], 16)

            def carry_wait():
                pool.sem_inc(pool_passed, 1)

            pool.wait_ge(tables_ready, 1)
            for s in range(2):
                pick_rows(gather_at, s, s)
            pool.wait_ge(rows_stored[0], 16 * IC * (PAIRS // 2))
            pool.wait_ge(rows_stored[1], 16 * IC * (PAIRS // 2))
            pool.wait_ge(pad_stored, 64)
            pool.wait_ge(picked, 2)
            for s in range(2):
                gather(s)
            rest_of(1, 0)
            rest_of(1, 1)
            pool.wait_ge(out_set, 16 * IC * NG)

            def tile_step(t, s, r, expert=None):
                more = not (isinstance(t, int) and t + 2 >= TILES)
                pick_rows(scatter_at, t, s)
                if more:
                    pool.wait_ge(gathered[s], 16 * SUB * (r + 1))
                    pool.wait_ge(x_ready, t + 1)
                    pick_rows(gather_at, t + 2, s)
                    pool.wait_ge(picked, 2 * t + 4)
                    carry_wait()
                    gather(s)
                else:
                    pool.wait_ge(picked, 2 * (TILES - 2) + 2 + t - (TILES - 2) + 1)
                if expert is not None:
                    rest_of(expert, 0)
                    rest_of(expert, 1)
                pool.wait_ge(y_ready, t + 1)
                if not (isinstance(t, int) and t == 0):
                    pool.wait_ge(added, 16 * SUB * t)
                carry_wait()
                for m in range(SUB):
                    pool.indirect_dma_start(
                        out=out, out_offset=numbers(scatter_at[:, s, m:m + 1]),
                        in_=y_out[:, s, m, :], in_offset=None, compute_op=ALU.add,
                    ).then_inc(added, 16)

            for t in range(FIRST):
                tile_step(t, t % 2, t // 2, t + 2 if t + 2 < E else None)
            with pool.Fori(0, ROUNDS) as r:
                for i in range(2):
                    tile_step(r * 2 + (FIRST + i), (FIRST + i) % 2, r + (FIRST + i) // 2)
            for t in range(TILES - 2, TILES):
                tile_step(t, t % 2, t // 2)
            pool.wait_ge(added, 16 * SUB * TILES)

        @block.scalar
        def _(act):
            act.wait_ge(consts_ready, 1)
            for m in range(SUB):
                pad = slice(T + m * P, T + (m + 1) * P)
                act.dma_start(rows_dram[pad, :], zero_row).then_inc(pad_stored, 16)
                act.dma_start(out[pad, :], zero_row[:, 0:D]).then_inc(pad_stored, 16)
            act.wait_ge(norm_ready, 1)
            nc.scalar.activation(root[:, :, :], norm[:, :, :], ACT.Sqrt).then_inc(root_ready, 1)
            for h in range(2):
                act.wait_ge(gt_done, h + 1)
                nc.scalar.copy(gt_sb[:, h, :], ps_gt[h][:, :]).then_inc(gt_taken, 1)
            act.wait_ge(shifted_ready, 1)
            nc.scalar.activation(probs[:, :, :], tmp[:, :, :], ACT.Exp).then_inc(exp_ready, 1)
            act.wait_ge(dn_ready, 1)
            for n in range(PAIRS):
                k = n % 2
                act.wait_ge(cond_done, n + 1)
                if n >= 2:
                    act.wait_ge(rows_stored[k], 16 * IC * (n // 2))
                for c in range(IC):
                    for j in range(2):
                        b = 2 * n + j
                        last = nc.scalar.activation(rows_out[:, k, c, j, 0:D],
                                                    ps_cond[k][c][:, j * D:(j + 1) * D],
                                                    ACT.Copy, scale=dn[:, c, b:b + 1])
                last.then_inc(cond_out, 1)
                act.wait_ge(cond_out, n + 1)
                act.wait_ge(gates_put, n + 1)
                for c in range(IC):
                    dst = rows_dram[0:T, :].rearrange("(b c p) l -> c p b l", b=B, c=IC)
                    ins = act.dma_start(dst[c][:, 2 * n:2 * n + 2, :], rows_out[:, k, c, :, :])
                    ins.then_inc(rows_stored[k], 16)
            act.wait_ge(bias_in, 32)
            act.wait_ge(tables_ready, 1)

            def gelu_tile(t):
                e = act.value_load(expert_of[0:1, bass.ds(t, 1)], min_val=0, max_val=E - 1)
                for f in range(FC):
                    j = f // BF
                    if f % BF == 0:
                        act.wait_ge(hidden, BANKS * t + j + 1)
                        if not (isinstance(t, int) and t < 1):
                            act.wait_ge(h_ready, BANKS * (t - 1) + j + 1)
                    part = slice(f % BF * N, (f % BF + 1) * N)
                    nc.scalar.activation(act_h[:, j, part], ps_h[j][:, part], ACT.Gelu_apprx_tanh,
                                         bias=b1_sb[:, bass.ds(e * FC + f, 1)]).then_inc(gelu_done, 1)

            gelu_tile(0)
            with act.Fori(1, TILES) as t:
                gelu_tile(t)

        @block.vector
        def _(dve):
            steps = [0]

            def step(ins):
                steps[0] += 1
                ins.then_inc(dve_step, 1)
                dve.wait_ge(dve_step, steps[0])

            v = nc.vector

            def over_e(ap):
                return ap.unsqueeze(2).to_broadcast([P, Q, E])

            dve.wait_ge(small_in, 48)
            v.tensor_tensor(cw_sq[:, :, :], cw[:, :, :], cw[:, :, :], ALU.mult)
            v.tensor_tensor(y_sq[:, :, :], y_sb[:, :, :], y_sb[:, :, :], ALU.mult).then_inc(sq_ready, 1)
            dve.wait_ge(norm_done, 1)
            v.tensor_scalar(norm[:, :, :], ps_norm, COND_SCALE * COND_SCALE, 1e-8,
                            ALU.mult, ALU.add).then_inc(norm_ready, 1)
            dve.wait_ge(root_ready, 1)
            step(v.reciprocal(dn[:, :, :], root[:, :, :]))
            step(v.tensor_tensor(newton[:, :, :], dn[:, :, :], dn[:, :, :], ALU.mult))
            step(v.tensor_tensor(newton[:, :, :], newton[:, :, :], norm[:, :, :], ALU.mult))
            step(v.tensor_scalar(newton[:, :, :], newton[:, :, :], -0.5 * COND_SCALE,
                                 1.5 * COND_SCALE, ALU.mult, ALU.add))
            steps[0] += 1
            v.tensor_tensor(dn[:, :, :], dn[:, :, :], newton[:, :, :], ALU.mult).then_inc(dve_step, 1)
            dve.wait_ge(dve_step, steps[0])
            for h in range(2):
                dve.wait_ge(g_done, h + 1)
                for c in range(IC):
                    by = slice(8 * h, 8 * (h + 1))
                    y_v = y_sb[:, c, by].rearrange("p (j b) -> p b j", b=2)
                    last = v.tensor_tensor(
                        yg[:, c, by, :].rearrange("p (j b) e -> p b j e", b=2),
                        ps_g[h][:, :, c, :, 0:E],
                        y_v.unsqueeze(3).to_broadcast([P, 2, 4, E]), ALU.mult)
                last.then_inc(yg_ready, 1)

            def head_of(e, k):
                dve.wait_ge(w_in[k], 16 * (e + 1))
                v.tensor_scalar(half(w_hi, e, k), stage[:, k, :], F16_MAX, -F16_MAX,
                                ALU.min, ALU.max).then_inc(head_done, 1)

            dve.wait_ge(logits_done, 1)
            dn_q = dn[:, :, :].rearrange("p c b -> p (c b)")
            dve.wait_ge(consts_ready, 1)
            step(v.tensor_tensor(logits[:, :, :], ps_log.rearrange("p c (b e) -> p (c b) e", e=E),
                                 over_e(dn_q), ALU.mult))
            rev_q = rev[:, :].unsqueeze(1).to_broadcast([P, Q, E])
            step(v.tensor_reduce(top[:, :], logits[:, :, :], AX.X, ALU.max))
            v.tensor_tensor(tmp[:, :, :], logits[:, :, :], over_e(top[:, :]),
                            ALU.subtract).then_inc(shifted_ready, 1)
            step(v.tensor_tensor(first[:, :, :], logits[:, :, :], over_e(top[:, :]), ALU.is_equal))
            step(v.tensor_tensor(first[:, :, :], first[:, :, :], rev_q, ALU.mult))
            step(v.tensor_reduce(pick[:, :], first[:, :, :], AX.X, ALU.max))
            step(v.tensor_tensor(first[:, :, :], over_e(pick[:, :]), rev_q, ALU.is_equal))
            step(v.scalar_tensor_tensor(logits[:, :, :], first[:, :, :], VERY_LOW, logits[:, :, :],
                                        ALU.mult, ALU.add))
            step(v.tensor_reduce(top[:, :], logits[:, :, :], AX.X, ALU.max))
            step(v.tensor_tensor(second[:, :, :], logits[:, :, :], over_e(top[:, :]), ALU.is_equal))
            step(v.tensor_tensor(second[:, :, :], second[:, :, :], rev_q, ALU.mult))
            step(v.tensor_reduce(pick[:, :], second[:, :, :], AX.X, ALU.max))
            step(v.tensor_tensor(second[:, :, :], over_e(pick[:, :]), rev_q, ALU.is_equal))
            v.tensor_tensor(both[:, :, :].rearrange("p e q -> p q e"), first[:, :, :],
                            second[:, :, :], ALU.add).then_inc(both_ready, 1)
            dve.wait_ge(exp_ready, 1)
            step(v.tensor_reduce(total[:, :], probs[:, :, :], AX.X, ALU.add))
            step(v.reciprocal(total[:, :], total[:, :]))
            step(v.tensor_tensor(tmp[:, :, :], first[:, :, :], second[:, :, :], ALU.add))
            step(v.tensor_tensor(tmp[:, :, :], tmp[:, :, :], probs[:, :, :], ALU.mult))
            step(v.tensor_tensor(g_all[:, :, :], tmp[:, :, :], over_e(total[:, :]), ALU.mult))
            v.tensor_copy(empty[:, 0:1], ones[:, 0:1]).then_inc(dn_ready, 1)
            g_v = g_all[:, :, :].rearrange("p (c b) e -> p c b e", c=IC)

            def put_gates(n):
                if n >= 2:
                    dve.wait_ge(rows_stored[n % 2], 32 * (n // 2))
                v.tensor_copy(rows_out[:, n % 2, :, :, D:ROW],
                              g_v[:, :, 2 * n:2 * n + 2, :]).then_inc(gates_put, 1)

            put_gates(0)
            put_gates(1)
            head_of(0, 0)
            head_of(0, 1)
            dve.wait_ge(prefix_done, 1)
            count = ps_count.rearrange("p (e q) -> p e q", e=E)
            step(v.tensor_tensor_scan(upto[:, :, :].rearrange("p e q -> p (e q)"),
                                      not_first[:, :, :].rearrange("p e q -> p (e q)"),
                                      ps_count, 0.0, ALU.mult, ALU.add))
            step(v.tensor_scalar(count_i[:, :], upto[:, :, Q - 1], float(N - 1), None, ALU.add))
            step(v.tensor_scalar(count_i[:, :], count_i[:, :], N.bit_length() - 1, None,
                                 ALU.logical_shift_right))
            step(v.tensor_scalar(n_tiles[:, :], count_i[:, :], 1.0, None, ALU.max))
            step(v.tensor_tensor_scan(end_tile[:, :], ones[:, :], n_tiles[:, :], 0.0,
                                      ALU.mult, ALU.add))
            step(v.tensor_tensor(base[:, :], end_tile[:, :], n_tiles[:, :], ALU.subtract))
            step(v.tensor_tensor(slot_e[:, :, :], upto[:, :, :], count, ALU.subtract))
            step(v.tensor_tensor(slot_e[:, :, :], slot_e[:, :, :],
                                 ps_before.rearrange("p (e q) -> p e q", e=E), ALU.add))
            step(v.scalar_tensor_tensor(slot_e[:, :, :],
                                        base[:, :].unsqueeze(2).to_broadcast([P, E, Q]), float(N),
                                        slot_e[:, :, :], ALU.mult, ALU.add))
            slot_q = slot_e[:, :, :].rearrange("p e q -> p q e")
            for k, chosen in enumerate((first, second)):
                step(v.tensor_tensor(tmp[:, :, :], slot_q, chosen[:, :, :], ALU.mult))
                step(v.tensor_reduce(slots[:, k, :], tmp[:, :, :], AX.X, ALU.add))
            step(v.tensor_copy(slots_i[:, :], slots[:, :, :].rearrange("p k q -> p (k q)")))
            v.tensor_scalar(part_i[:, 0, :], slots_i[:, :], 7, None, ALU.logical_shift_right)
            step(v.tensor_scalar(part_i[:, 1, :], slots_i[:, :], P - 1, None, ALU.bitwise_and))
            step(v.tensor_copy(part_f[:, :, :], part_i[:, :, :]))
            put_gates(2)
            v.tensor_tensor(lo_hot, col[:, :].unsqueeze(1).to_broadcast([P, J, P]),
                            part_f[:, 1, :].unsqueeze(2).to_broadcast([P, J, P]), ALU.is_equal)
            put_gates(3)
            step(v.tensor_tensor(hi_hot, col[:, 0:U].unsqueeze(1).to_broadcast([P, J, U]),
                                 part_f[:, 0, :].unsqueeze(2).to_broadcast([P, J, U]),
                                 ALU.is_equal))
            for k in range(TOP):
                q = slice(k * Q, (k + 1) * Q)
                last = v.tensor_tensor(hi_tile[:, q, :], hi_hot[:, q, :],
                                       tile_at[:, :].unsqueeze(2).to_broadcast([P, Q, U]), ALU.mult)
            step(last)
            v.tensor_scalar(hi_hot, hi_hot, row[:, 0:1], None, ALU.mult).then_inc(hots_ready, 1)
            for n in range(4, PAIRS):
                put_gates(n)
            dve.wait_ge(slots_done, 1)
            step(v.scalar_tensor_tensor(empty[:, :], ps_rows, 0.0, pad_row[:, :],
                                        ALU.is_equal, ALU.mult))
            v.scalar_tensor_tensor(rows_of[:, :], ps_rows, float(T), empty[:, :], ALU.add, ALU.add)
            step(v.tensor_tensor(ended[:, :, :],
                                 end_tile[0:1, 0:E - 1].unsqueeze(1).to_broadcast([1, TILES, E - 1]),
                                 col[0:1, 0:TILES].unsqueeze(2).to_broadcast([1, TILES, E - 1]),
                                 ALU.is_le))
            step(v.tensor_reduce(expert_of_f[:, :], ended[:, :, :], AX.X, ALU.add))
            v.tensor_copy(expert_of[:, :], expert_of_f[:, :]).then_inc(tables_ready, 1)

            head_of(1, 0)
            head_of(1, 1)

            def split_x(t, s):
                e = dve.value_load(expert_of[0:1, bass.ds(t, 1)], min_val=0, max_val=E - 1)
                dve.wait_ge(turned, t + 1)
                if not (isinstance(t, int) and t < 1):
                    dve.wait_ge(hidden, BANKS * t)
                v.tensor_scalar(x_hi[:, :, :].rearrange("p c n -> p (c n)"), ps_xt, F16_MAX,
                                -F16_MAX, ALU.min, ALU.max).then_inc(x_head, 1)
                v.tensor_copy(gates[:, s, :, :], x_rows[:, s, :, bass.ds(D + e, 1)])
                if isinstance(t, int):
                    dve.wait_ge(rest_done, 2 * min(t + 1, E))
                dve.wait_ge(x_head, t + 1)
                v.tensor_tensor(x_lo[:, :, :].rearrange("p c n -> p (c n)"), ps_xt,
                                x_hi[:, :, :].rearrange("p c n -> p (c n)"),
                                ALU.subtract).then_inc(x_ready, 1)

            def split_h(t, j):
                dve.wait_ge(gelu_done, FC * t + BF * (j + 1))
                if j == 0 and not (isinstance(t, int) and t < 1):
                    dve.wait_ge(down_done, t)
                f = slice(j * BF, (j + 1) * BF)
                a = act_h[:, j, :].rearrange("p (f n) -> p f n", n=N)
                v.tensor_scalar(h_hi[:, f, :], a, F16_MAX, -F16_MAX,
                                ALU.min, ALU.max).then_inc(h_head, 1)
                dve.wait_ge(h_head, BANKS * t + j + 1)
                v.tensor_tensor(h_lo[:, f, :], a, h_hi[:, f, :], ALU.subtract).then_inc(h_ready, 1)

            def finish_y(t, s):
                e = dve.value_load(expert_of[0:1, bass.ds(t, 1)], min_val=0, max_val=E - 1)
                dve.wait_ge(down_done, t + 1)
                for m in range(SUB):
                    v.tensor_tensor(y_sum[:, m, :], ps_y[m], b2_sb[:, bass.ds(e * D, D)],
                                    ALU.add).then_inc(y_taken, 1)
                if not (isinstance(t, int) and t < 2):
                    dve.wait_ge(added, 16 * SUB * (t - 1))
                dve.wait_ge(y_taken, SUB * (t + 1))
                for m in range(SUB):
                    last = v.tensor_scalar(y_out[:, s, m, :], y_sum[:, m, :], gates[:, s, m, 0:1],
                                           None, ALU.mult)
                last.then_inc(y_ready, 1)

            def tile_step(t, s, expert=None):
                if not (isinstance(t, int) and t == 0):
                    finish_y(t - 1, 1 - s)
                for j in range(BANKS):
                    split_h(t, j)
                if not (isinstance(t, int) and t + 1 >= TILES):
                    split_x(t + 1, 1 - s)
                if expert is not None:
                    head_of(expert, 0)
                    head_of(expert, 1)

            dve.wait_ge(bias_in, 32)
            dve.wait_ge(tables_ready, 1)
            split_x(0, 0)
            for t in range(FIRST):
                tile_step(t, t % 2, t + 2 if t + 2 < E else None)
            with dve.Fori(0, ROUNDS) as r:
                for i in range(2):
                    tile_step(r * 2 + (FIRST + i), (FIRST + i) % 2)
            for t in range(TILES - 2, TILES):
                tile_step(t, t % 2)
            finish_y(TILES - 1, (TILES - 1) % 2)

        @block.tensor
        def _(pe):
            mm = nc.tensor.matmul
            pe.wait_ge(sq_ready, 1)
            for o in range(IC):
                for c in range(IC):
                    last = mm(ps_norm[:, o, :], cw_sq[:, c, o * P:(o + 1) * P], y_sq[:, c, :],
                              start=(c == 0), stop=(c == IC - 1))
            last.then_inc(norm_done, 1)
            for h in range(2):
                for j in range(4):
                    n = 4 * h + j
                    if n % 2 == 0:
                        pe.wait_ge(xt_in[n // 2], 16 * DC)
                    for c in range(DC):
                        last = mm(ps_gt[h][GW * j:GW * (j + 1), :], gw[:, c, :],
                                  xt_sb[:, c, 2 * n:2 * n + 2, :].rearrange("p b i -> p (b i)"),
                                  start=(c == 0), stop=(c == DC - 1))
                last.then_inc(gt_done, 1)
            pe.wait_ge(consts_ready, 1)
            pe.wait_ge(norm_ready, 1)
            for h in range(2):
                pe.wait_ge(gt_taken, h + 1)
                for k in range(4):
                    last = nc.tensor.transpose(bank[2 + h][:, k * P:(k + 1) * P],
                                               gt_sb[:, h, k * P:(k + 1) * P], ident[:, :])
                last.then_inc(g_done, 1)
            pe.wait_ge(yg_ready, 2)
            for o in range(IC):
                for c in range(IC):
                    last = mm(ps_log[:, o, :], cw[:, c, o * P:(o + 1) * P],
                              yg[:, c, :, :].rearrange("p b e -> p (b e)"),
                              start=(c == 0), stop=(c == IC - 1))
            last.then_inc(logits_done, 1)

            def cond_pair(n):
                pe.wait_ge(xs_ready, n + 1)
                if n >= 2:
                    pe.wait_ge(cond_out, n - 1)
                for o in range(IC):
                    for c in range(IC):
                        last = mm(ps_cond[n % 2][o][:, :], cw[:, c, o * P:(o + 1) * P],
                                  xs[:, n % 2, c, :], start=(c == 0), stop=(c == IC - 1))
                last.then_inc(cond_done, 1)

            cond_pair(0)
            cond_pair(1)
            pe.wait_ge(both_ready, 1)
            pe.wait_ge(consts_ready, 1)
            both_f = both[:, :, :].rearrange("p e q -> p (e q)")
            mm(ps_before, before[:, :], both_f, start=True, stop=True)
            mm(ps_count, ones_bf[:, :], both_f, start=True, stop=True).then_inc(prefix_done, 1)
            for n in range(2, PAIRS):
                cond_pair(n)
            pe.wait_ge(hots_ready, 1)
            for j in range(J):
                for part in (hi_tile, hi_hot):
                    last = mm(ps_rows, lo_hot[:, j, :], part[:, j, :],
                              start=(j == 0 and part is hi_tile), stop=(j == J - 1 and part is hi_hot))
            last.then_inc(slots_done, 1)
            pe.wait_ge(tables_ready, 1)

            def turn(t, s, r):
                pe.wait_ge(gathered[s], 16 * SUB * (r + 1))
                if not (isinstance(t, int) and t < 1):
                    pe.wait_ge(x_ready, t)
                for c in range(DC):
                    for m in range(SUB):
                        last = nc.tensor.transpose(ps_xt[:, c * N + m * P:c * N + (m + 1) * P],
                                                   x_rows[:, s, m, c * P:(c + 1) * P], ident[:, :])
                last.then_inc(turned, 1)

            def up(t):
                e = pe.value_load(expert_of[0:1, bass.ds(t, 1)], min_val=0, max_val=E - 1)
                pe.wait_ge(x_ready, t + 1)
                for f in range(FC):
                    j = f // BF
                    if f % BF == 0 and not (isinstance(t, int) and t < 1):
                        pe.wait_ge(gelu_done, FC * (t - 1) + BF * (j + 1))
                    to = ps_h[j][:, f % BF * N:(f % BF + 1) * N]
                    for c in range(DC):
                        at = bass.ds(e * WC + (c * F + f * P), P)
                        mm(to, w_hi[:, at], x_hi[:, c, :], start=(c == 0), stop=False)
                        mm(to, w_hi[:, at], x_lo[:, c, :], start=False, stop=False)
                        last = mm(to, w_lo[:, at], x_hi[:, c, :], start=False, stop=(c == DC - 1))
                    if f % BF == BF - 1:
                        last.then_inc(hidden, 1)
                return e

            def down(t, e):
                if not (isinstance(t, int) and t < 1):
                    pe.wait_ge(y_taken, SUB * t)
                for f in range(FC):
                    if f % BF == 0:
                        pe.wait_ge(h_ready, BANKS * t + f // BF + 1)
                    at = bass.ds(e * WC + (W1C + f * D), D)
                    for m in range(SUB):
                        rows = slice(m * P, (m + 1) * P)
                        mm(ps_y[m], h_hi[:, f, rows], w_hi[:, at], start=(f == 0), stop=False)
                        mm(ps_y[m], h_hi[:, f, rows], w_lo[:, at], start=False, stop=False)
                        last = mm(ps_y[m], h_lo[:, f, rows], w_hi[:, at], start=False,
                                  stop=(f == FC - 1))
                last.then_inc(down_done, 1)

            def tile_step(t, s, r):
                e = up(t)
                if not (isinstance(t, int) and t + 1 >= TILES):
                    turn(t + 1, 1 - s, r)
                down(t, e)

            turn(0, 0, 0)
            tile_step(0, 0, 0)
            with pe.Fori(0, (TILES - 3) // 2) as r:
                tile_step(r * 2 + 1, 1, r + 1)
                tile_step(r * 2 + 2, 0, r + 1)
            for t in range(TILES - 2, TILES):
                tile_step(t, t % 2, (t + 1) // 2)


def kernel(x, cond_1024, L0_cond_weight, L0_ffn_gate_w, L0_ffn_w1, L0_ffn_b1, L0_ffn_w2, L0_ffn_b2):
    import numpy as np
    import concourse.bacc as bacc
    from concourse.bass_utils import run_bass_kernel_spmd

    x = np.asarray(x)
    B, S, D = x.shape
    E, F = L0_ffn_b1.shape
    w1, w2 = np.asarray(L0_ffn_w1), np.asarray(L0_ffn_w2)
    arrays = {
        "x": x,
        "x_t": x.transpose(0, 2, 1),
        "y_t": np.asarray(cond_1024).T.reshape(S // P, P, B),
        "cond_w_t": np.asarray(L0_cond_weight)[0, :, :, 0].T.reshape(S // P, P, S),
        "gate_w_t": np.asarray(L0_ffn_gate_w).T.reshape(D // P, P, E),
        "w1": w1.transpose(1, 2, 0).reshape(E, D // P, P, F).transpose(0, 2, 1, 3),
        "b1": np.asarray(L0_ffn_b1).reshape(E, F // P, P).transpose(2, 0, 1).reshape(P, -1),
        "w2": w2.transpose(1, 2, 0).reshape(E, F // P, P, D).transpose(0, 2, 1, 3),
        "b2": np.asarray(L0_ffn_b2).reshape(-1),
    }
    nc = bacc.Bacc("TRN2", target_bir_lowering=False, num_devices=1)
    ins, aps = {}, []
    for name, a in arrays.items():
        a = np.ascontiguousarray(a)
        ins[f"in_{name}"] = a
        aps.append(nc.dram_tensor(f"in_{name}", a.shape, mybir.dt.from_np(a.dtype),
                                  kind="ExternalInput").ap())
    out = nc.dram_tensor("out", (B * S + 2 * P, D), F32, kind="ExternalOutput").ap()
    moe_kernel(nc, *aps, out)
    got = run_bass_kernel_spmd(nc, [ins], core_ids=[0]).results[0]["out"]
    return got[:B * S].reshape(B, S, D)
```

```python
from contextlib import ExitStack

import concourse.bass as bass
from concourse import mybir

P = 128
ALU = mybir.AluOpType
ACT = mybir.ActivationFunctionType
AX = mybir.AxisListType
F32 = mybir.dt.float32
F16 = mybir.dt.float16
BF16 = mybir.dt.bfloat16
I32 = mybir.dt.int32
F16_MAX = 65504.0
VERY_LOW = -3.0e38


def moe_kernel(nc, x, x_t, y_t, cond_w_t, gate_w_t, w1, b1, w2, b2, out):
    B, S, D = x.shape
    E = gate_w_t.shape[2]
    F = w1.shape[3]
    IC = S // P
    DC = D // P
    FC = F // P
    T = B * S
    Q = T // P
    TOP = 2
    SUB = 2
    N = SUB * P
    TILES = (TOP * T + E * (N - 1)) // N
    SURE = TOP * T // N
    U = TILES * SUB
    UX = U + 2 * SUB
    ROW = D + E
    W1C = DC * F
    WC = W1C + FC * D
    PIECES = 4
    POOL_PIECES = 3
    GROUP = 4
    NG = B // GROUP
    PAIRS = B // 2
    POOL_PAIRS = 6
    BF = 512 // N
    BANKS = FC // BF
    GW = 32
    WARM = 17
    COND_SCALE = 1.0 / float(S) ** 0.5

    with ExitStack() as ctx:

        def sb(name, shape, dt):
            return ctx.enter_context(nc.sbuf_tensor(name, shape, dt))

        def sem(name):
            return ctx.enter_context(nc.semaphore(name))

        w_hi = sb("w_hi", [P, E * WC], F16)
        w_lo = sb("w_lo", [P, E * WC], BF16)
        xt_sb = w_hi[:, E // 2 * WC:].bitcast(F32).rearrange("p (c b i) -> p c b i", c=DC, b=B)
        x_sb = w_lo[:, E // 2 * WC:].bitcast(F32).rearrange("p (c b l) -> p c b l", c=IC, b=B)
        HOTS = E // 2 * WC
        J = TOP * Q

        def hots(start, n):
            return w_hi[:, HOTS + J * start:HOTS + J * (start + n)].rearrange("p (j n) -> p j n", n=n)

        tokens_hot, lo_hot = hots(0, U), hots(U, P)
        stage = sb("stage", [P, PIECES, WC // PIECES], F32)

        x_rows = sb("x_rows", [P, 2, SUB, ROW], F32)
        x_hi = sb("x_hi", [P, DC, N], F16)
        x_lo = sb("x_lo", [P, DC, N], BF16)
        gates = sb("gates", [P, 2, SUB, 1], F32)
        act_h = sb("act_h", [P, BANKS, BF * N], F32)
        h_area = sb("h_area", [P, 2 * IC * 2 * ROW], F32)
        h_hi = h_area[:, 0:F * SUB // 2].bitcast(F16).rearrange("p (f n) -> p f n", n=N)
        h_lo = h_area[:, F * SUB // 2:F * SUB].bitcast(BF16).rearrange("p (f n) -> p f n", n=N)
        y_sum = sb("y_sum", [P, SUB, D], F32)
        y_out = sb("y_out", [P, 2, SUB, D], F32)
        gather_at = sb("gather_at", [P, 2, SUB], I32)
        scatter_at = sb("scatter_at", [P, 2, SUB], I32)
        b1_sb = sb("b1_sb", [P, E * FC], F32)
        b2_sb = sb("b2_sb", [P, E * D], F32)
        xs = act_h[:, :, :].rearrange("p (k c) n -> p k c n", k=2)
        rows_out = h_area[:, :].rearrange("p (k c j n) -> p k c j n", k=2, c=IC, j=2)

        cw = sb("cw", [P, IC, S], F32)
        cw_sq = y_out[:, 0, :, :]
        gw = sb("gw", [P, DC, GW], F32)
        gt_sb = sb("gt_sb", [P, 2, 512], F32)
        y_sb = sb("y_sb", [P, IC, B], F32)
        y_sq = sb("y_sq", [P, IC, B], F32)
        yg = sb("yg", [P, IC, B, E], F32)
        norm = sb("norm", [P, IC, B], F32)
        root = sb("root", [P, IC, B], F32)
        newton = sb("newton", [P, IC, B], F32)
        dn = sb("dn", [P, IC, B], F32)

        logits = sb("logits", [P, Q, E], F32)
        probs = sb("probs", [P, Q, E], F32)
        tmp = sb("tmp", [P, Q, E], F32)
        first = sb("first", [P, Q, E], F32)
        second = sb("second", [P, Q, E], F32)
        both = sb("both", [P, E, Q], BF16)
        top = sb("top", [P, Q], F32)
        pick = sb("pick", [P, Q], F32)
        total = sb("total", [P, Q], F32)
        g_all = sb("g_all", [P, Q, E], F32)
        upto = sb("upto", [P, E, Q], F32)
        slot_e = sb("slot_e", [P, E, Q], F32)
        count_i = sb("count_i", [P, E], I32)
        n_tiles = sb("n_tiles", [P, E], F32)
        end_tile = sb("end_tile", [P, E], F32)
        base = sb("base", [P, E], F32)
        slots = sb("slots", [P, TOP, Q], F32)
        slots_i = sb("slots_i", [P, TOP * Q], I32)
        part_i = sb("part_i", [P, 2, TOP * Q], I32)
        part_h = sb("part_h", [P, 2, TOP * Q], F16)
        empty = sb("empty", [P, U], F32)
        above = sb("above", [P, U], F32)
        gelu_first = sb("gelu_first", [P, 1], F32)
        rows_of = sb("rows_of", [P, UX], I32)
        pad_row = sb("pad_row", [P, U], F32)
        ended = x_rows[0:1, 0, :, :].rearrange("p s n -> p (s n)")[:, 0:(TILES + 1) * (E - 1)].rearrange(
            "p (t e) -> p t e", e=E - 1)
        expert_of_f = sb("expert_of_f", [1, TILES + 1], F32)
        expert_of = sb("expert_of", [1, TILES + 1], I32)
        used = sb("used", [1, 1], I32)

        ident = sb("ident", [P, P], F32)
        before = sb("before", [P, P], BF16)
        ones_bf = sb("ones_bf", [P, P], BF16)
        ones = sb("ones", [P, E], F32)
        zero_row = y_sum[:, :, :].rearrange("p s n -> p (s n)")[:, 0:ROW]
        rev = sb("rev", [P, E], F32)
        col = sb("col", [P, P], F32)
        col16 = sb("col16", [P, P], F16)
        payload = sb("payload", [P, Q], F16)
        not_first = sb("not_first", [P, E, Q], F32)

        rows_dram = nc.dram_tensor("rows_dram", [T + N, ROW], F32, kind="Internal").ap()

        bank = [ctx.enter_context(nc.psum_tensor(f"bank{i}", [P, 512], F32)) for i in range(8)]
        ps_gt = [bank[h] for h in range(2)]
        ps_g = [bank[2 + h][:, :].rearrange("p (b c j e) -> p b c j e", b=2, c=IC, j=4) for h in range(2)]
        ps_norm = bank[3][:, 0:IC * B].rearrange("p (c b) -> p c b", c=IC)
        ps_log = bank[0][:, 0:IC * B * E].rearrange("p (c n) -> p c n", c=IC)
        ps_before = bank[1][:, 0:E * Q]
        ps_count = bank[1][:, E * Q:2 * E * Q]
        ps_rows = bank[2][:, 0:U]
        ps_cond = [[bank[4 + 2 * k + c] for c in range(IC)] for k in range(2)]
        ps_h = [bank[j] for j in range(BANKS)]
        ps_xt = bank[4][:, 0:DC * N]
        ps_y = [bank[6 + m][:, 0:D] for m in range(SUB)]

        small_in = sem("small_in")
        xt_in = [sem(f"xt_in{i}") for i in range(NG)]
        x_in = [sem(f"x_in{i}") for i in range(NG)]
        b1_in = sem("b1_in")
        b2_in = sem("b2_in")
        w_in = [sem(f"w_in{i}") for i in range(PIECES)]
        gw_set = sem("gw_set")
        head_done = [sem(f"head_done{i}") for i in range(PIECES)]
        rest_done = [sem(f"rest_done{i}") for i in range(PIECES)]
        consts_ready = sem("consts_ready")
        pool_step = sem("pool_step")
        dve_step = sem("dve_step")
        sq_ready = sem("sq_ready")
        norm_done = sem("norm_done")
        norm_ready = sem("norm_ready")
        root_ready = sem("root_ready")
        gt_done = sem("gt_done")
        gt_taken = sem("gt_taken")
        g_done = sem("g_done")
        yg_ready = sem("yg_ready")
        logits_done = sem("logits_done")
        shifted_ready = sem("shifted_ready")
        exp_ready = sem("exp_ready")
        gates_ready = sem("gates_ready")
        pool_xs = sem("pool_xs")
        act_xs = sem("act_xs")
        cond_done = sem("cond_done")
        cond_out = sem("cond_out")
        gates_out = sem("gates_out")
        rows_stored = [sem(f"rows_stored{k}") for k in range(2)]
        pad_stored = sem("pad_stored")
        out_set = sem("out_set")
        both_ready = sem("both_ready")
        prefix_done = sem("prefix_done")
        gather_hots = sem("gather_hots")
        token_hots = sem("token_hots")
        place_hots = sem("place_hots")
        slots_done = sem("slots_done")
        tables_ready = sem("tables_ready")

        pool_passed = sem("pool_passed")
        picked = sem("picked")
        gathered = [sem(f"gathered{s}") for s in range(2)]
        turned = sem("turned")
        x_head = sem("x_head")
        x_ready = sem("x_ready")
        hidden = sem("hidden")
        gelu_done = sem("gelu_done")
        h_head = sem("h_head")
        h_ready = sem("h_ready")
        down_done = sem("down_done")
        y_taken = sem("y_taken")
        y_ready = sem("y_ready")
        added = sem("added")

        FIRST = E - 1
        ROUNDS = (SURE - 1 - FIRST) // 2
        LAST = FIRST + 2 * ROUNDS
        LAST_ROUNDS = (TILES - LAST) // 2
        assert LAST + 2 * LAST_ROUNDS == TILES and LAST < SURE

        block = ctx.enter_context(nc.Block())

        def piece(t, e, i):
            width = WC // PIECES
            return t[:, e * WC + i * width:e * WC + (i + 1) * width]

        def rest_of(engine, ops, e, i):
            engine.wait_ge(head_done[i], e + 1)
            ops.tensor_tensor(piece(w_lo, e, i), stage[:, i, :], piece(w_hi, e, i),
                              ALU.subtract).then_inc(rest_done[i], 1)

        @block.sync
        def _(sp):
            sp.wait_ge(gw_set, 1)
            sp.dma_start(gw[:, :, 0:E], gate_w_t.rearrange("c p e -> p c e")).then_inc(small_in, 16)
            sp.dma_start(y_sb[:, :, :], y_t.rearrange("c p b -> p c b")).then_inc(small_in, 16)
            sp.dma_start(cw[:, :, :], cond_w_t.rearrange("c p o -> p c o")).then_inc(small_in, 16)

            def samples(g):
                return slice(g * GROUP, (g + 1) * GROUP)

            def load_x(g):
                for c in range(IC):
                    sp.dma_start(x_sb[:, c, samples(g), :], x[samples(g), c * P:(c + 1) * P, :].rearrange(
                        "b p l -> p b l")).then_inc(x_in[g], 16)

            def load_w(e, k):
                src = (w1, w2)[k][e].rearrange("p a b -> p (a b)")
                n = PIECES // 2
                width = WC // PIECES
                for i in range(n):
                    if e > 0:
                        sp.wait_ge(rest_done[k * n + i], e)
                    sp.dma_start(stage[:, k * n + i, :],
                                 src[:, i * width:(i + 1) * width]).then_inc(w_in[k * n + i], 16)

            for g in range(NG):
                for c in range(DC):
                    sp.dma_start(xt_sb[:, c, samples(g), :], x_t[samples(g), c * P:(c + 1) * P, :].rearrange(
                        "b p i -> p b i")).then_inc(xt_in[g], 16)
            for g in range(NG // 2):
                load_x(g)
            load_w(0, 0)
            for g in range(NG // 2, NG):
                load_x(g)
            rows = rows_dram[0:T, :].rearrange("(b c p) l -> c p b l", b=B, c=IC)
            out_rows = out[0:T, :].rearrange("(b c p) l -> c p b l", b=B, c=IC)
            def init_out(n):
                for c in range(IC):
                    pair = slice(2 * n, 2 * n + 2)
                    sp.dma_start(out_rows[c][:, pair, :], x_sb[:, c, pair, :]).then_inc(out_set, 16)

            for n in range(PAIRS):
                sp.wait_ge(cond_out, n + 1)
                sp.wait_ge(gates_out, n + 1)
                for c in range(IC):
                    sp.dma_start(rows[c][:, 2 * n:2 * n + 2, :],
                                 rows_out[:, n % 2, c, :, :]).then_inc(rows_stored[n % 2], 16)
                if n == 0:
                    init_out(0)
                if n == 1:
                    load_w(0, 1)
                if n == 2:
                    sp.wait_ge(consts_ready, 1)
                    for m in range(SUB):
                        pad = slice(T + m * P, T + (m + 1) * P)
                        sp.dma_start(rows_dram[pad, :], zero_row).then_inc(pad_stored, 16)
                        sp.dma_start(out[pad, :], zero_row[:, 0:D]).then_inc(pad_stored, 16)
                    sp.dma_start(b1_sb[:, :], b1).then_inc(b1_in, 16)
                if n == 3:
                    load_w(1, 0)
            sp.wait_ge(gathered[0], 16 * SUB)
            load_w(1, 1)
            sp.dma_start(b2_sb[:, :], b2.partition_broadcast(P)).then_inc(b2_in, 16)
            for n in range(1, PAIRS):
                init_out(n)
            for e in range(2, E):
                load_w(e, 0)
                load_w(e, 1)

        @block.gpsimd
        def _(pool):
            steps = [0]

            def step(ins):
                steps[0] += 1
                ins.then_inc(pool_step, 1)
                pool.wait_ge(pool_step, steps[0])

            pool.memset(gw[:, :, :], 0.0).then_inc(gw_set, 1)
            pool.memset(ident[:, :], 0.0)
            pool.memset(ones_bf[:, :], 1.0)
            pool.memset(ones[:, :], 1.0)
            pool.memset(not_first[:, :, :], 1.0)
            step(pool.memset(zero_row, 0.0))
            pool.iota(col[:, :], [[1, P]], base=0, channel_multiplier=0,
                      allow_small_or_imprecise_dtypes=True)
            pool.iota(col16[:, :], [[1, P]], base=0, channel_multiplier=0,
                      allow_small_or_imprecise_dtypes=True)
            for h in range(2):
                samples = slice(h * B // 2, (h + 1) * B // 2)
                pool.iota(payload[:, :].rearrange("p (c b) -> p c b", c=IC)[:, :, samples],
                          [[P, IC], [S, B // 2]], base=-T // 2 if h == 0 else 1,
                          channel_multiplier=1, allow_small_or_imprecise_dtypes=True)
            pool.iota(pad_row[:, :], [[0, TILES], [P, SUB]], base=T // 2, channel_multiplier=1,
                      allow_small_or_imprecise_dtypes=True)
            pool.iota(rows_of[:, U:UX], [[0, 2], [P, SUB]], base=T, channel_multiplier=1)
            pool.iota(rev[:, :], [[-1, E]], base=E, channel_multiplier=0,
                      allow_small_or_imprecise_dtypes=True)
            pool.memset(not_first[:, :, 0:1], 0.0)
            pool.affine_select(out=ident[:, :], in_=ident[:, :], compare_op=ALU.not_equal, fill=1.0,
                               base=0, pattern=[[-1, P]], channel_multiplier=1)
            step(pool.affine_select(out=before[:, :], in_=ones_bf[:, :], compare_op=ALU.is_gt,
                                    fill=0.0, base=0, pattern=[[1, P]], channel_multiplier=-1))
            pool.memset(gates[:, :, :, :], 0.0).then_inc(consts_ready, 1)
            pool.wait_ge(small_in, 48)

            def scale_pair(n):
                if n % 2 == 0:
                    pool.wait_ge(x_in[n // 2], 16 * IC)
                if n >= 2:
                    pool.wait_ge(cond_done, n - 1)
                for k in range(2):
                    b = 2 * n + k
                    last = pool.tensor_scalar(xs[:, n % 2, 1, k * D:(k + 1) * D],
                                              x_sb[:, 1, b, :], y_sb[:, 1, b:b + 1], 1.0,
                                              ALU.mult, ALU.mult)
                last.then_inc(pool_xs, 1)

            for n in range(4):
                scale_pair(n)
            rest_of(pool, pool, 0, 0)
            rest_of(pool, pool, 0, 1)
            scale_pair(4)
            scale_pair(5)
            for k in range(TOP):
                pool.wait_ge(gather_hots, k + 1)
                hot = tokens_hot[:, k * Q:(k + 1) * Q, :]
                pool.tensor_tensor(hot, hot, payload[:, :].unsqueeze(2).to_broadcast([P, Q, U]),
                                   ALU.mult).then_inc(token_hots, 1)
            rest_of(pool, pool, 0, 2)

            def pick_rows(to, t, s):
                pool.tensor_copy(to[:, s, :], rows_of[:, bass.ds(t * SUB, SUB)]).then_inc(picked, 1)

            def numbers(ap):
                return bass.IndirectOffsetOnAxis(ap=ap.bitcast(mybir.dt.uint32), axis=0)

            def gather(s):
                for m in range(SUB):
                    pool.indirect_dma_start(
                        out=x_rows[:, s, m, :], out_offset=None, in_=rows_dram,
                        in_offset=numbers(gather_at[:, s, m:m + 1])).then_inc(gathered[s], 16)

            def carry_wait():
                pool.sem_inc(pool_passed, 1)

            pool.wait_ge(tables_ready, 1)
            for s in range(2):
                pick_rows(gather_at, s, s)
            pool.wait_ge(rows_stored[0], 16 * IC * (PAIRS // 2))
            pool.wait_ge(rows_stored[1], 16 * IC * (PAIRS // 2))
            pool.wait_ge(pad_stored, 64)
            pool.wait_ge(picked, 2)
            for s in range(2):
                gather(s)

            def tile_step(t, s, r, expert=None):
                pick_rows(scatter_at, t, s)
                pool.wait_ge(gathered[s], 16 * SUB * (r + 1))
                pool.wait_ge(x_ready, t + 1)
                pick_rows(gather_at, t + 2, s)
                pool.wait_ge(picked, 2 * t + 4)
                carry_wait()
                gather(s)
                if expert is not None:
                    for i in range(POOL_PIECES):
                        rest_of(pool, pool, expert, i)
                pool.wait_ge(y_ready, t + 1)
                if isinstance(t, int) and t == 0:
                    pool.wait_ge(out_set, 16 * IC * PAIRS)
                if not (isinstance(t, int) and t == 0):
                    pool.wait_ge(added, 16 * SUB * t)
                carry_wait()
                for m in range(SUB):
                    pool.indirect_dma_start(
                        out=out, out_offset=numbers(scatter_at[:, s, m:m + 1]),
                        in_=y_out[:, s, m, :], in_offset=None, compute_op=ALU.add,
                    ).then_inc(added, 16)

            for t in range(FIRST):
                tile_step(t, t % 2, t // 2, t + 1)
            with pool.Fori(0, ROUNDS) as r:
                for i in range(2):
                    tile_step(r * 2 + (FIRST + i), (FIRST + i) % 2, r + (FIRST + i) // 2)
            tiles = pool.value_load(used[0:1, 0:1], min_val=SURE, max_val=TILES)
            with pool.Fori(0, LAST_ROUNDS) as r:
                for i in range(2):
                    t = r * 2 + (LAST + i)
                    with pool.If(t < tiles):
                        tile_step(t, (LAST + i) % 2, r + (LAST + i) // 2)
                        pool.wait_ge(added, 16 * SUB * (t + 1))
            for s in range(2):
                pool.wait_ge(gathered[s], ((tiles + (3 - s)) >> 1) * (16 * SUB))
                carry_wait()

        @block.scalar
        def _(act):
            act.wait_ge(norm_ready, 1)
            nc.scalar.activation(root[:, :, :], norm[:, :, :], ACT.Sqrt).then_inc(root_ready, 1)
            for h in range(2):
                act.wait_ge(gt_done, h + 1)
                nc.scalar.copy(gt_sb[:, h, :], ps_gt[h][:, :]).then_inc(gt_taken, 1)
            act.wait_ge(small_in, 48)

            def scale_pair(n):
                if n % 2 == 0:
                    act.wait_ge(x_in[n // 2], 16 * IC)
                if n >= 2:
                    act.wait_ge(cond_done, n - 1)
                for c in range(1 if n < POOL_PAIRS else IC):
                    for j in range(2):
                        b = 2 * n + j
                        last = nc.scalar.activation(xs[:, n % 2, c, j * D:(j + 1) * D],
                                                    x_sb[:, c, b, :], ACT.Copy,
                                                    scale=y_sb[:, c, b:b + 1])
                last.then_inc(act_xs, 1)

            scale_pair(0)
            scale_pair(1)
            act.wait_ge(shifted_ready, 1)
            nc.scalar.activation(probs[:, :, :], tmp[:, :, :], ACT.Exp).then_inc(exp_ready, 1)
            nc.scalar.activation(gelu_first[:, :], ones[:, 0:1], ACT.Gelu_apprx_tanh)
            g_v = g_all[:, :, :].rearrange("p (c b) e -> p c b e", c=IC)
            for n in range(PAIRS):
                k = n % 2
                pair = slice(2 * n, 2 * n + 2)
                if n + 2 < PAIRS:
                    scale_pair(n + 2)
                act.wait_ge(cond_done, n + 1)
                if n >= 2:
                    act.wait_ge(rows_stored[k], 16 * IC * (n // 2))
                for c in range(IC):
                    for j in range(2):
                        b = 2 * n + j
                        last = nc.scalar.activation(rows_out[:, k, c, j, 0:D],
                                                    ps_cond[k][c][:, j * D:(j + 1) * D],
                                                    ACT.Copy, scale=dn[:, c, b:b + 1])
                last.then_inc(cond_out, 1)
                if n == 0:
                    act.wait_ge(gates_ready, 1)
                nc.scalar.copy(rows_out[:, k, :, :, D:ROW], g_v[:, :, pair, :]).then_inc(gates_out, 1)
            act.wait_ge(b1_in, 16)
            act.wait_ge(tables_ready, 1)

            def gelu_tile(t):
                e = act.value_load(expert_of[0:1, bass.ds(t, 1)], min_val=0, max_val=E - 1)
                for f in range(FC):
                    j = f // BF
                    if f % BF == 0:
                        act.wait_ge(hidden, BANKS * t + j + 1)
                        if not (isinstance(t, int) and t < 1):
                            act.wait_ge(h_ready, BANKS * (t - 1) + j + 1)
                    part = slice(f % BF * N, (f % BF + 1) * N)
                    nc.scalar.activation(act_h[:, j, part], ps_h[j][:, part], ACT.Gelu_apprx_tanh,
                                         bias=b1_sb[:, bass.ds(e * FC + f, 1)]).then_inc(gelu_done, 1)

            gelu_tile(0)
            with act.Fori(1, LAST) as t:
                gelu_tile(t)
            tiles = act.value_load(used[0:1, 0:1], min_val=SURE, max_val=TILES)
            with act.Fori(LAST, TILES) as t:
                with act.If(t < tiles):
                    gelu_tile(t)

        @block.vector
        def _(dve):
            steps = [0]

            def step(ins):
                steps[0] += 1
                ins.then_inc(dve_step, 1)
                dve.wait_ge(dve_step, steps[0])

            v = nc.vector

            def over_e(ap):
                return ap.unsqueeze(2).to_broadcast([P, Q, E])

            dve.wait_ge(small_in, 48)
            v.tensor_tensor(cw_sq[:, :, :], cw[:, :, :], cw[:, :, :], ALU.mult)
            v.tensor_tensor(y_sq[:, :, :], y_sb[:, :, :], y_sb[:, :, :], ALU.mult).then_inc(sq_ready, 1)
            dve.wait_ge(norm_done, 1)
            v.tensor_scalar(norm[:, :, :], ps_norm, COND_SCALE * COND_SCALE, 1e-8,
                            ALU.mult, ALU.add).then_inc(norm_ready, 1)
            dve.wait_ge(root_ready, 1)
            step(v.reciprocal(dn[:, :, :], root[:, :, :]))
            step(v.tensor_tensor(newton[:, :, :], dn[:, :, :], dn[:, :, :], ALU.mult))
            step(v.tensor_tensor(newton[:, :, :], newton[:, :, :], norm[:, :, :], ALU.mult))
            step(v.tensor_scalar(newton[:, :, :], newton[:, :, :], -0.5 * COND_SCALE,
                                 1.5 * COND_SCALE, ALU.mult, ALU.add))
            steps[0] += 1
            v.tensor_tensor(dn[:, :, :], dn[:, :, :], newton[:, :, :], ALU.mult).then_inc(dve_step, 1)
            dve.wait_ge(dve_step, steps[0])
            for h in range(2):
                dve.wait_ge(g_done, h + 1)
                for c in range(IC):
                    by = slice(8 * h, 8 * (h + 1))
                    y_v = y_sb[:, c, by].rearrange("p (j b) -> p b j", b=2)
                    last = v.tensor_tensor(
                        yg[:, c, by, :].rearrange("p (j b) e -> p b j e", b=2),
                        ps_g[h][:, :, c, :, 0:E],
                        y_v.unsqueeze(3).to_broadcast([P, 2, 4, E]), ALU.mult)
                last.then_inc(yg_ready, 1)

            def head_of(e, i):
                dve.wait_ge(w_in[i], 16 * (e + 1))
                v.tensor_scalar(piece(w_hi, e, i), stage[:, i, :], F16_MAX, -F16_MAX,
                                ALU.min, ALU.max).then_inc(head_done[i], 1)

            dve.wait_ge(logits_done, 1)
            dn_q = dn[:, :, :].rearrange("p c b -> p (c b)")
            dve.wait_ge(consts_ready, 1)
            step(v.tensor_tensor(logits[:, :, :], ps_log.rearrange("p c (b e) -> p (c b) e", e=E),
                                 over_e(dn_q), ALU.mult))
            rev_q = rev[:, :].unsqueeze(1).to_broadcast([P, Q, E])
            step(v.tensor_reduce(top[:, :], logits[:, :, :], AX.X, ALU.max))
            v.tensor_tensor(tmp[:, :, :], logits[:, :, :], over_e(top[:, :]),
                            ALU.subtract).then_inc(shifted_ready, 1)
            step(v.tensor_tensor(first[:, :, :], logits[:, :, :], over_e(top[:, :]), ALU.is_equal))
            step(v.tensor_tensor(first[:, :, :], first[:, :, :], rev_q, ALU.mult))
            step(v.tensor_reduce(pick[:, :], first[:, :, :], AX.X, ALU.max))
            step(v.tensor_tensor(first[:, :, :], over_e(pick[:, :]), rev_q, ALU.is_equal))
            step(v.scalar_tensor_tensor(logits[:, :, :], first[:, :, :], VERY_LOW, logits[:, :, :],
                                        ALU.mult, ALU.add))
            step(v.tensor_reduce(top[:, :], logits[:, :, :], AX.X, ALU.max))
            step(v.tensor_tensor(second[:, :, :], logits[:, :, :], over_e(top[:, :]), ALU.is_equal))
            step(v.tensor_tensor(second[:, :, :], second[:, :, :], rev_q, ALU.mult))
            step(v.tensor_reduce(pick[:, :], second[:, :, :], AX.X, ALU.max))
            step(v.tensor_tensor(second[:, :, :], over_e(pick[:, :]), rev_q, ALU.is_equal))
            v.tensor_tensor(both[:, :, :].rearrange("p e q -> p q e"), first[:, :, :],
                            second[:, :, :], ALU.add).then_inc(both_ready, 1)
            dve.wait_ge(exp_ready, 1)
            step(v.tensor_reduce(total[:, :], probs[:, :, :], AX.X, ALU.add))
            step(v.reciprocal(total[:, :], total[:, :]))
            step(v.tensor_tensor(tmp[:, :, :], first[:, :, :], second[:, :, :], ALU.add))
            step(v.tensor_tensor(tmp[:, :, :], tmp[:, :, :], probs[:, :, :], ALU.mult))
            v.tensor_tensor(g_all[:, :, :], tmp[:, :, :], over_e(total[:, :]),
                            ALU.mult).then_inc(gates_ready, 1)
            head_of(0, 0)
            head_of(0, 1)
            dve.wait_ge(prefix_done, 1)
            count = ps_count.rearrange("p (e q) -> p e q", e=E)
            step(v.tensor_tensor_scan(upto[:, :, :].rearrange("p e q -> p (e q)"),
                                      not_first[:, :, :].rearrange("p e q -> p (e q)"),
                                      ps_count, 0.0, ALU.mult, ALU.add))
            step(v.tensor_scalar(count_i[:, :], upto[:, :, Q - 1], float(N - 1), None, ALU.add))
            step(v.tensor_scalar(count_i[:, :], count_i[:, :], N.bit_length() - 1, None,
                                 ALU.logical_shift_right))
            step(v.tensor_scalar(n_tiles[:, :], count_i[:, :], 1.0, None, ALU.max))
            step(v.tensor_tensor_scan(end_tile[:, :], ones[:, :], n_tiles[:, :], 0.0,
                                      ALU.mult, ALU.add))
            step(v.tensor_tensor(base[:, :], end_tile[:, :], n_tiles[:, :], ALU.subtract))
            step(v.tensor_tensor(slot_e[:, :, :], upto[:, :, :], count, ALU.subtract))
            step(v.tensor_tensor(slot_e[:, :, :], slot_e[:, :, :],
                                 ps_before.rearrange("p (e q) -> p e q", e=E), ALU.add))
            step(v.scalar_tensor_tensor(slot_e[:, :, :],
                                        base[:, :].unsqueeze(2).to_broadcast([P, E, Q]), float(N),
                                        slot_e[:, :, :], ALU.mult, ALU.add))
            slot_q = slot_e[:, :, :].rearrange("p e q -> p q e")
            for k, chosen in enumerate((first, second)):
                step(v.tensor_tensor(tmp[:, :, :], slot_q, chosen[:, :, :], ALU.mult))
                step(v.tensor_reduce(slots[:, k, :], tmp[:, :, :], AX.X, ALU.add))
            step(v.tensor_copy(slots_i[:, :], slots[:, :, :].rearrange("p k q -> p (k q)")))
            v.tensor_scalar(part_i[:, 0, :], slots_i[:, :], 7, None, ALU.logical_shift_right)
            step(v.tensor_scalar(part_i[:, 1, :], slots_i[:, :], P - 1, None, ALU.bitwise_and))
            step(v.tensor_copy(part_h[:, :, :], part_i[:, :, :]))
            for k in range(TOP):
                q = slice(k * Q, (k + 1) * Q)
                v.tensor_tensor(tokens_hot[:, q, :], col16[:, 0:U].unsqueeze(1).to_broadcast([P, Q, U]),
                                part_h[:, 0, q].unsqueeze(2).to_broadcast([P, Q, U]),
                                ALU.is_equal).then_inc(gather_hots, 1)
            for k in range(TOP):
                q = slice(k * Q, (k + 1) * Q)
                v.tensor_tensor(lo_hot[:, q, :], col16[:, :].unsqueeze(1).to_broadcast([P, Q, P]),
                                part_h[:, 1, q].unsqueeze(2).to_broadcast([P, Q, P]),
                                ALU.is_equal).then_inc(place_hots, 1)
            head_of(0, 2)
            head_of(0, 3)
            rest_of(dve, v, 0, 3)
            dve.wait_ge(slots_done, 1)
            step(v.scalar_tensor_tensor(empty[:, :], ps_rows, 0.0, pad_row[:, :],
                                        ALU.is_equal, ALU.mult))
            step(v.tensor_scalar(above[:, :], ps_rows, 0.0, -1.0, ALU.is_gt, ALU.mult))
            step(v.tensor_tensor(empty[:, :], empty[:, :], above[:, :], ALU.add))
            v.scalar_tensor_tensor(rows_of[:, 0:U], ps_rows, float(T // 2), empty[:, :],
                                   ALU.add, ALU.add)
            step(v.tensor_tensor(ended[:, :, :],
                                 end_tile[0:1, 0:E - 1].unsqueeze(1).to_broadcast([1, TILES + 1, E - 1]),
                                 col[0:1, 0:TILES + 1].unsqueeze(2).to_broadcast([1, TILES + 1, E - 1]),
                                 ALU.is_le))
            v.tensor_copy(used[:, :], end_tile[0:1, E - 1:E])
            step(v.tensor_reduce(expert_of_f[:, :], ended[:, :, :], AX.X, ALU.add))
            v.tensor_copy(expert_of[:, :], expert_of_f[:, :]).then_inc(tables_ready, 1)

            def weights_complete(k, t, e):
                for i in range(k * PIECES // 2, (k + 1) * PIECES // 2):
                    dve.wait_ge(rest_done[i], e + 1 if isinstance(t, int) else E)

            def split_x(t, s):
                e = dve.value_load(expert_of[0:1, bass.ds(t, 1)], min_val=0, max_val=E - 1)
                dve.wait_ge(turned, t + 1)
                if not (isinstance(t, int) and t < 1):
                    dve.wait_ge(hidden, BANKS * t)
                v.tensor_scalar(x_hi[:, :, :].rearrange("p c n -> p (c n)"), ps_xt, F16_MAX,
                                -F16_MAX, ALU.min, ALU.max).then_inc(x_head, 1)
                v.tensor_copy(gates[:, s, :, :], x_rows[:, s, :, bass.ds(D + e, 1)])
                weights_complete(0, t, e)
                dve.wait_ge(x_head, t + 1)
                v.tensor_tensor(x_lo[:, :, :].rearrange("p c n -> p (c n)"), ps_xt,
                                x_hi[:, :, :].rearrange("p c n -> p (c n)"),
                                ALU.subtract).then_inc(x_ready, 1)

            def split_h(t, j):
                if j == 0:
                    e = None
                    if isinstance(t, int):
                        e = dve.value_load(expert_of[0:1, bass.ds(t, 1)], min_val=0, max_val=E - 1)
                    weights_complete(1, t, e)
                dve.wait_ge(gelu_done, FC * t + BF * (j + 1))
                if j == 0 and not (isinstance(t, int) and t < 1):
                    dve.wait_ge(down_done, t)
                f = slice(j * BF, (j + 1) * BF)
                a = act_h[:, j, :].rearrange("p (f n) -> p f n", n=N)
                v.tensor_scalar(h_hi[:, f, :], a, F16_MAX, -F16_MAX,
                                ALU.min, ALU.max).then_inc(h_head, 1)
                dve.wait_ge(h_head, BANKS * t + j + 1)
                v.tensor_tensor(h_lo[:, f, :], a, h_hi[:, f, :], ALU.subtract).then_inc(h_ready, 1)

            def finish_y(t, s):
                e = dve.value_load(expert_of[0:1, bass.ds(t, 1)], min_val=0, max_val=E - 1)
                dve.wait_ge(down_done, t + 1)
                if isinstance(t, int) and t == 0:
                    dve.wait_ge(b2_in, 16)
                for m in range(SUB):
                    v.tensor_tensor(y_sum[:, m, :], ps_y[m], b2_sb[:, bass.ds(e * D, D)],
                                    ALU.add).then_inc(y_taken, 1)
                if not (isinstance(t, int) and t < 2):
                    dve.wait_ge(added, 16 * SUB * (t - 1))
                dve.wait_ge(y_taken, SUB * (t + 1))
                for m in range(SUB):
                    last = v.tensor_scalar(y_out[:, s, m, :], y_sum[:, m, :], gates[:, s, m, 0:1],
                                           None, ALU.mult)
                last.then_inc(y_ready, 1)

            def tile_step(t, s, expert=None):
                for j in range(BANKS):
                    split_h(t, j)
                if expert is not None:
                    head_of(expert, 0)
                    head_of(expert, 1)
                split_x(t + 1, 1 - s)
                if expert is not None:
                    head_of(expert, 2)
                    head_of(expert, 3)
                    rest_of(dve, v, expert, 3)
                finish_y(t, s)

            dve.wait_ge(tables_ready, 1)
            split_x(0, 0)
            for t in range(FIRST):
                tile_step(t, t % 2, t + 1)
            with dve.Fori(0, ROUNDS) as r:
                for i in range(2):
                    tile_step(r * 2 + (FIRST + i), (FIRST + i) % 2)
            tiles = dve.value_load(used[0:1, 0:1], min_val=SURE, max_val=TILES)
            with dve.Fori(0, LAST_ROUNDS) as r:
                for i in range(2):
                    t = r * 2 + (LAST + i)
                    with dve.If(t < tiles):
                        tile_step(t, (LAST + i) % 2)

        @block.tensor
        def _(pe):
            mm = nc.tensor.matmul
            pe.wait_ge(sq_ready, 1)
            for o in range(IC):
                for c in range(IC):
                    last = mm(ps_norm[:, o, :], cw_sq[:, c, o * P:(o + 1) * P], y_sq[:, c, :],
                              start=(c == 0), stop=(c == IC - 1))
            last.then_inc(norm_done, 1)
            for h in range(2):
                for j in range(4):
                    n = 4 * h + j
                    if n % 2 == 0:
                        pe.wait_ge(xt_in[n // 2], 16 * DC)
                    for c in range(DC):
                        last = mm(ps_gt[h][GW * j:GW * (j + 1), :], gw[:, c, :],
                                  xt_sb[:, c, 2 * n:2 * n + 2, :].rearrange("p b i -> p (b i)"),
                                  start=(c == 0), stop=(c == DC - 1))
                last.then_inc(gt_done, 1)
                if h == 0:
                    pe.wait_ge(consts_ready, 1)
                else:
                    pe.wait_ge(norm_ready, 1)
                pe.wait_ge(gt_taken, h + 1)
                for k in range(4):
                    last = nc.tensor.transpose(bank[2 + h][:, k * P:(k + 1) * P],
                                               gt_sb[:, h, k * P:(k + 1) * P], ident[:, :])
                last.then_inc(g_done, 1)
            pe.wait_ge(yg_ready, 2)
            for o in range(IC):
                for c in range(IC):
                    last = mm(ps_log[:, o, :], cw[:, c, o * P:(o + 1) * P],
                              yg[:, c, :, :].rearrange("p b e -> p (b e)"),
                              start=(c == 0), stop=(c == IC - 1))
            last.then_inc(logits_done, 1)

            def cond_pair(n):
                pe.wait_ge(act_xs, n + 1)
                if n < POOL_PAIRS:
                    pe.wait_ge(pool_xs, n + 1)
                if n >= 2:
                    pe.wait_ge(cond_out, n - 1)
                for o in range(IC):
                    for c in range(IC):
                        last = mm(ps_cond[n % 2][o][:, :], cw[:, c, o * P:(o + 1) * P],
                                  xs[:, n % 2, c, :], start=(c == 0), stop=(c == IC - 1))
                last.then_inc(cond_done, 1)

            cond_pair(0)
            cond_pair(1)
            pe.wait_ge(both_ready, 1)
            pe.wait_ge(consts_ready, 1)
            both_f = both[:, :, :].rearrange("p e q -> p (e q)")
            mm(ps_before, before[:, :], both_f, start=True, stop=True)
            mm(ps_count, ones_bf[:, :], both_f, start=True, stop=True).then_inc(prefix_done, 1)
            for n in range(2, PAIRS):
                cond_pair(n)
            for j in range(J):
                if j % Q == 0:
                    pe.wait_ge(token_hots, j // Q + 1)
                    pe.wait_ge(place_hots, j // Q + 1)
                last = mm(ps_rows, lo_hot[:, j, :], tokens_hot[:, j, :], start=(j == 0),
                          stop=(j == J - 1))
            last.then_inc(slots_done, 1)
            pe.wait_ge(tables_ready, 1)
            idle = lo_hot[:, 0:4, :].rearrange("p j n -> p (j n)")
            for i in range(WARM):
                mm(bank[0][:, :], ones_bf[:, :], idle, start=(i == 0), stop=(i == WARM - 1))

            def turn(t, s, r):
                pe.wait_ge(gathered[s], 16 * SUB * (r + 1))
                if not (isinstance(t, int) and t < 1):
                    pe.wait_ge(x_ready, t)
                for c in range(DC):
                    for m in range(SUB):
                        last = nc.tensor.transpose(ps_xt[:, c * N + m * P:c * N + (m + 1) * P],
                                                   x_rows[:, s, m, c * P:(c + 1) * P], ident[:, :])
                last.then_inc(turned, 1)

            def up(t):
                e = pe.value_load(expert_of[0:1, bass.ds(t, 1)], min_val=0, max_val=E - 1)
                pe.wait_ge(x_ready, t + 1)
                for f in range(FC):
                    j = f // BF
                    if f % BF == 0 and not (isinstance(t, int) and t < 1):
                        pe.wait_ge(gelu_done, FC * (t - 1) + BF * (j + 1))
                    to = ps_h[j][:, f % BF * N:(f % BF + 1) * N]
                    for c in range(DC):
                        at = bass.ds(e * WC + (c * F + f * P), P)
                        mm(to, w_hi[:, at], x_hi[:, c, :], start=(c == 0), stop=False)
                        mm(to, w_hi[:, at], x_lo[:, c, :], start=False, stop=False)
                        last = mm(to, w_lo[:, at], x_hi[:, c, :], start=False, stop=(c == DC - 1))
                    if f % BF == BF - 1:
                        last.then_inc(hidden, 1)
                return e

            def down(t, e):
                if not (isinstance(t, int) and t < 1):
                    pe.wait_ge(y_taken, SUB * t)
                for f in range(FC):
                    if f % BF == 0:
                        pe.wait_ge(h_ready, BANKS * t + f // BF + 1)
                    at = bass.ds(e * WC + (W1C + f * D), D)
                    for m in range(SUB):
                        rows = slice(m * P, (m + 1) * P)
                        mm(ps_y[m], h_hi[:, f, rows], w_hi[:, at], start=(f == 0), stop=False)
                        mm(ps_y[m], h_hi[:, f, rows], w_lo[:, at], start=False, stop=False)
                        last = mm(ps_y[m], h_lo[:, f, rows], w_hi[:, at], start=False,
                                  stop=(f == FC - 1))
                last.then_inc(down_done, 1)

            def tile_step(t, s, r):
                e = up(t)
                turn(t + 1, 1 - s, r)
                down(t, e)

            turn(0, 0, 0)
            tile_step(0, 0, 0)
            with pe.Fori(0, (LAST - 1) // 2) as r:
                tile_step(r * 2 + 1, 1, r + 1)
                tile_step(r * 2 + 2, 0, r + 1)
            tiles = pe.value_load(used[0:1, 0:1], min_val=SURE, max_val=TILES)
            with pe.Fori((LAST - 1) // 2, (TILES - 1) // 2) as r:
                for i in range(2):
                    t = r * 2 + (1 + i)
                    with pe.If(t < tiles):
                        tile_step(t, 1 - i, r + 1)


def kernel(x, cond_1024, L0_cond_weight, L0_ffn_gate_w, L0_ffn_w1, L0_ffn_b1, L0_ffn_w2, L0_ffn_b2):
    import numpy as np
    import concourse.bacc as bacc
    from concourse.bass_utils import run_bass_kernel_spmd

    x = np.asarray(x)
    B, S, D = x.shape
    E, F = L0_ffn_b1.shape
    w1, w2 = np.asarray(L0_ffn_w1), np.asarray(L0_ffn_w2)
    arrays = {
        "x": x,
        "x_t": x.transpose(0, 2, 1),
        "y_t": np.asarray(cond_1024).T.reshape(S // P, P, B),
        "cond_w_t": np.asarray(L0_cond_weight)[0, :, :, 0].T.reshape(S // P, P, S),
        "gate_w_t": np.asarray(L0_ffn_gate_w).T.reshape(D // P, P, E),
        "w1": w1.transpose(1, 2, 0).reshape(E, D // P, P, F).transpose(0, 2, 1, 3),
        "b1": np.asarray(L0_ffn_b1).reshape(E, F // P, P).transpose(2, 0, 1).reshape(P, -1),
        "w2": w2.transpose(1, 2, 0).reshape(E, F // P, P, D).transpose(0, 2, 1, 3),
        "b2": np.asarray(L0_ffn_b2).reshape(-1),
    }
    nc = bacc.Bacc("TRN2", target_bir_lowering=False, num_devices=1)
    ins, aps = {}, []
    for name, a in arrays.items():
        a = np.ascontiguousarray(a)
        ins[f"in_{name}"] = a
        aps.append(nc.dram_tensor(f"in_{name}", a.shape, mybir.dt.from_np(a.dtype),
                                  kind="ExternalInput").ap())
    out = nc.dram_tensor("out", (B * S + 2 * P, D), F32, kind="ExternalOutput").ap()
    moe_kernel(nc, *aps, out)
    got = run_bass_kernel_spmd(nc, [ins], core_ids=[0]).results[0]["out"]
    return got[:B * S].reshape(B, S, D)
```
